# Optimizing a Trainium2 kernel written in Bass

```python
import numpy as np
import jax
import jax.numpy as jnp

def _softmax(x, axis=-1):
    return jax.nn.softmax(x, axis=axis)

def _gelu(x):
    return jax.nn.gelu(x, approximate=True)

def _silu(x):
    return jax.nn.silu(x)

def _sigmoid(x):
    return jax.nn.sigmoid(x)

def _layernorm(x, axis=-1, eps=1e-05):
    m = jnp.mean(x, axis=axis, keepdims=True)
    v = jnp.var(x, axis=axis, keepdims=True)
    return (x - m) / jnp.sqrt(v + eps)

def _scatter_add(tgt, idx, src, axis=0):
    return tgt.at[idx].add(src)

def _segment_sum(src, seg, n):
    return jax.ops.segment_sum(src, seg, n)
kernel_name = 'mk_metaformer_d2_conv_nchw512_r4_996d38'

def setup_inputs(seed: int=0):
    np.random.seed(seed)
    _w = jnp.asarray

    def _rec_inputs():
        import jax
        import jax.numpy as jnp
        _gk = jax.random.key(seed)
        x = -0.0002928 + 1 * jax.random.normal(jax.random.fold_in(_gk, 1), (2, 128, 16, 16), jnp.float32)
        return x
    x = _rec_inputs()

    def _L0_conv_setup():
        import jax, jax.numpy as jnp
        import numpy as np
        DIM, D_STATE, EXPAND, D_CONV = (128, 16, 2, 4)
        D_INNER = EXPAND * DIM
        DT_RANK = (DIM + 15) // 16
        EPS = 1e-05

        def _clamp(x):
            return jnp.clip(x, -10.0, 10.0)

        def _layernorm(x, w, b):
            mu = x.mean(-1, keepdims=True)
            var = x.var(-1, keepdims=True)
            return (x - mu) * jax.lax.rsqrt(var + EPS) * w + b
        key = jax.random.key(seed)
        ks = jax.random.split(key, 8)
        B, H, W = (2, 16, 16)

        def rn(k, shape, s=0.02):
            return jax.random.normal(k, shape, jnp.float32) * s
        return {'x': jax.random.normal(ks[0], (B, DIM, H, W), jnp.float32), 'norm_w': jnp.ones((DIM,), jnp.float32), 'norm_b': jnp.zeros((DIM,), jnp.float32), 'in_proj_w': rn(ks[1], (2 * D_INNER, DIM)), 'conv_w': rn(ks[2], (D_INNER, 1, D_CONV), 0.1), 'conv_b': jnp.zeros((D_INNER,), jnp.float32), 'x_proj_w': rn(ks[3], (DT_RANK + 2 * D_STATE, D_INNER)), 'dt_proj_w': rn(ks[4], (D_INNER, DT_RANK), 0.1), 'dt_proj_b': jnp.log(jnp.expm1(jnp.full((D_INNER,), 0.01, jnp.float32))), 'A_log': jnp.log(jnp.broadcast_to(jnp.arange(1, D_STATE + 1, dtype=jnp.float32), (D_INNER, D_STATE))), 'D': jnp.ones((D_INNER,), jnp.float32), 'out_proj_w': rn(ks[5], (DIM, D_INNER))}
    _L0_conv_all = _L0_conv_setup()
    _L0_conv_in = {k: v for k, v in _L0_conv_all.items() if k in ('norm_w', 'norm_b', 'in_proj_w', 'conv_w', 'conv_b', 'x_proj_w', 'dt_proj_w', 'dt_proj_b', 'A_log', 'D', 'out_proj_w')}
    del _L0_conv_all

    def _L0_ffn_setup():
        import jax, jax.numpy as jnp
        import numpy as np
        NUM_EXPERTS = 8
        TOP_K = 2
        LN_EPS = 1e-05

        def _layernorm(x, g, b):
            mu = jnp.mean(x, axis=-1, keepdims=True)
            var = jnp.mean(jnp.square(x - mu), axis=-1, keepdims=True)
            return (x - mu) * jax.lax.rsqrt(var + LN_EPS) * g + b
        key = jax.random.key(seed)
        ks = jax.random.split(key, 8)
        B, S, D, F, E = (8, 1024, 128, 512, NUM_EXPERTS)
        return {'x': jax.random.normal(ks[0], (B, S, D), dtype=jnp.float32), 'gate_w': jax.random.normal(ks[1], (D, E), dtype=jnp.float32) * 0.02, 'w1': jax.random.normal(ks[2], (E, D, F), dtype=jnp.float32) * 0.02, 'b1': jnp.zeros((E, F), dtype=jnp.float32), 'w2': jax.random.normal(ks[3], (E, F, D), dtype=jnp.float32) * 0.02, 'b2': jnp.zeros((E, D), dtype=jnp.float32), 'ln_g': jnp.ones((D,), dtype=jnp.float32), 'ln_b': jnp.zeros((D,), dtype=jnp.float32)}
    _L0_ffn_all = _L0_ffn_setup()
    _L0_ffn_in = {k: v for k, v in _L0_ffn_all.items() if k in ('gate_w', 'w1', 'b1', 'w2', 'b2', 'ln_g', 'ln_b')}
    del _L0_ffn_all

    def _L1_conv_setup():
        import jax, jax.numpy as jnp
        import numpy as np
        EPS = 1e-06
        key = jax.random.key(seed)
        k1, k2 = jax.random.split(key)
        b, seq, d = (4, 128, 16)
        x = jax.random.normal(k1, (b, seq, d, d), dtype=jnp.float32)
        A = jax.random.uniform(k2, (d,), dtype=jnp.float32)
        return {'x': x, 'A': A}
    _L1_conv_all = _L1_conv_setup()
    _L1_conv_in = {k: v for k, v in _L1_conv_all.items() if k in ('A',)}
    del _L1_conv_all

    def _L1_ffn_setup():
        import jax, jax.numpy as jnp
        import numpy as np
        K = 2
        key = jax.random.key(seed)
        k1, k2, k3, k4 = jax.random.split(key, 4)
        B, L, D, H, E = (8, 256, 128, 256, 16)
        x = jax.random.normal(k1, (B, L, D), dtype=jnp.float32)
        W_gate = jax.random.normal(k2, (D, E), dtype=jnp.float32) * 0.02
        W1 = jax.random.normal(k3, (E, D, H), dtype=jnp.float32) * 0.02
        W2 = jax.random.normal(k4, (E, H, D), dtype=jnp.float32) * 0.02
        return {'x': x, 'W_gate': W_gate, 'W1': W1, 'W2': W2}
    _L1_ffn_all = _L1_ffn_setup()
    _L1_ffn_in = {k: v for k, v in _L1_ffn_all.items() if k in ('W_gate', 'W1', 'W2')}
    del _L1_ffn_all
    return {'x': x, 'L0_conv_norm_w': _L0_conv_in['norm_w'], 'L0_conv_norm_b': _L0_conv_in['norm_b'], 'L0_conv_in_proj_w': _L0_conv_in['in_proj_w'], 'L0_conv_conv_w': _L0_conv_in['conv_w'], 'L0_conv_conv_b': _L0_conv_in['conv_b'], 'L0_conv_x_proj_w': _L0_conv_in['x_proj_w'], 'L0_conv_dt_proj_w': _L0_conv_in['dt_proj_w'], 'L0_conv_dt_proj_b': _L0_conv_in['dt_proj_b'], 'L0_conv_A_log': _L0_conv_in['A_log'], 'L0_conv_D': _L0_conv_in['D'], 'L0_conv_out_proj_w': _L0_conv_in['out_proj_w'], 'L0_ffn_gate_w': _L0_ffn_in['gate_w'], 'L0_ffn_w1': _L0_ffn_in['w1'], 'L0_ffn_b1': _L0_ffn_in['b1'], 'L0_ffn_w2': _L0_ffn_in['w2'], 'L0_ffn_b2': _L0_ffn_in['b2'], 'L0_ffn_ln_g': _L0_ffn_in['ln_g'], 'L0_ffn_ln_b': _L0_ffn_in['ln_b'], 'L1_conv_A': _L1_conv_in['A'], 'L1_ffn_W_gate': _L1_ffn_in['W_gate'], 'L1_ffn_W1': _L1_ffn_in['W1'], 'L1_ffn_W2': _L1_ffn_in['W2']}

def reference(x, L0_conv_norm_w, L0_conv_norm_b, L0_conv_in_proj_w, L0_conv_conv_w, L0_conv_conv_b, L0_conv_x_proj_w, L0_conv_dt_proj_w, L0_conv_dt_proj_b, L0_conv_A_log, L0_conv_D, L0_conv_out_proj_w, L0_ffn_gate_w, L0_ffn_w1, L0_ffn_b1, L0_ffn_w2, L0_ffn_b2, L0_ffn_ln_g, L0_ffn_ln_b, L1_conv_A, L1_ffn_W_gate, L1_ffn_W1, L1_ffn_W2):
    import jax
    import jax.numpy as jnp

    def _L0_conv_ref(x, norm_w, norm_b, in_proj_w, conv_w, conv_b, x_proj_w, dt_proj_w, dt_proj_b, A_log, D, out_proj_w):
        import jax, jax.numpy as jnp
        import numpy as np
        DIM, D_STATE, EXPAND, D_CONV = (128, 16, 2, 4)
        D_INNER = EXPAND * DIM
        DT_RANK = (DIM + 15) // 16
        EPS = 1e-05

        def _clamp(x):
            return jnp.clip(x, -10.0, 10.0)

        def _layernorm(x, w, b):
            mu = x.mean(-1, keepdims=True)
            var = x.var(-1, keepdims=True)
            return (x - mu) * jax.lax.rsqrt(var + EPS) * w + b
        B, C, H, W = x.shape
        L = H * W
        x = _clamp(x)
        xs = x.reshape(B, C, L).transpose(0, 2, 1)
        xs = _clamp(_layernorm(xs, norm_w, norm_b))
        xz = xs @ in_proj_w.T
        xin, z = jnp.split(xz, 2, axis=-1)
        xc = jax.lax.conv_general_dilated(xin.transpose(0, 2, 1), conv_w, (1,), [(D_CONV - 1, 0)], feature_group_count=D_INNER)
        xc = jax.nn.silu(xc + conv_b[None, :, None]).transpose(0, 2, 1)
        xdbl = xc @ x_proj_w.T
        dt = xdbl[..., :DT_RANK]
        Bm = xdbl[..., DT_RANK:DT_RANK + D_STATE]
        Cm = xdbl[..., DT_RANK + D_STATE:]
        dt = jax.nn.softplus(dt @ dt_proj_w.T + dt_proj_b)
        A = -jnp.exp(A_log)

        def step(h, inp):
            dt_t, B_t, C_t, x_t = inp
            dA = jnp.exp(dt_t[..., None] * A)
            h = dA * h + (dt_t * x_t)[..., None] * B_t[:, None, :]
            y = jnp.einsum('bdn,bn->bd', h, C_t)
            return (h, y)
        scan_xs = (dt.transpose(1, 0, 2), Bm.transpose(1, 0, 2), Cm.transpose(1, 0, 2), xc.transpose(1, 0, 2))
        h0 = jnp.zeros((B, D_INNER, D_STATE), xc.dtype)
        _, ys = jax.lax.scan(step, h0, scan_xs)
        y = ys.transpose(1, 0, 2) + xc * D
        y = y * jax.nn.silu(z)
        out = y @ out_proj_w.T
        out = _clamp(out)
        out = _layernorm(out, jnp.ones((C,), out.dtype), jnp.zeros((C,), out.dtype))
        out = out.transpose(0, 2, 1).reshape(B, C, H, W)
        return _clamp(out)

    def _L0_ffn_ref(x, gate_w, w1, b1, w2, b2, ln_g, ln_b):
        import jax, jax.numpy as jnp
        import numpy as np
        NUM_EXPERTS = 8
        TOP_K = 2
        LN_EPS = 1e-05

        def _layernorm(x, g, b):
            mu = jnp.mean(x, axis=-1, keepdims=True)
            var = jnp.mean(jnp.square(x - mu), axis=-1, keepdims=True)
            return (x - mu) * jax.lax.rsqrt(var + LN_EPS) * g + b
        B, S, D = x.shape
        E = gate_w.shape[1]
        x_norm = _layernorm(x, ln_g, ln_b)
        xf = x_norm.reshape(B * S, D)
        logits = xf @ gate_w
        probs = jax.nn.softmax(logits, axis=-1)
        dispatch_w, expert_idx = jax.lax.top_k(probs, TOP_K)
        combine = jnp.sum(jax.nn.one_hot(expert_idx, E, dtype=xf.dtype) * dispatch_w[..., None], axis=1)
        out = jnp.zeros_like(xf)
        for e in range(E):
            h = jax.nn.gelu(xf @ w1[e] + b1[e], approximate=False)
            y = h @ w2[e] + b2[e]
            out = out + combine[:, e:e + 1] * y
        return x + out.reshape(B, S, D)

    def _L1_conv_ref(x, A):
        import jax, jax.numpy as jnp
        import numpy as np
        EPS = 1e-06
        b, seq, d, _ = x.shape
        log_A = jnp.log(jnp.clip(A, EPS))
        cs_A = jnp.cumsum(jnp.broadcast_to(log_A, (seq, d)), axis=0)
        log_M = cs_A[:, None, :] - cs_A[None, :, :]
        idx = jnp.arange(seq)
        mask = idx[:, None] >= idx[None, :]
        M = jnp.where(mask[:, :, None], jnp.exp(log_M), 0.0)
        out = jnp.einsum('tjr,bjrc->btrc', M, x)
        return out

    def _L1_ffn_ref(x, W_gate, W1, W2):
        import jax, jax.numpy as jnp
        import numpy as np
        K = 2
        B, L, D = x.shape
        E = W_gate.shape[1]
        xf = x.reshape(-1, D)
        T = xf.shape[0]
        probs = jax.nn.softmax(xf @ W_gate, axis=-1)
        top_g, top_i = jax.lax.top_k(probs, K)
        gates = jnp.zeros((T, E), dtype=x.dtype).at[jnp.arange(T)[:, None], top_i].set(top_g)

        def step(y, params):
            W1e, W2e, ge = params
            h = jax.nn.gelu(xf @ W1e, approximate=False)
            return (y + ge[:, None] * (h @ W2e), None)
        y0 = jnp.zeros((T, D), dtype=x.dtype)
        y, _ = jax.lax.scan(step, y0, (W1, W2, gates.T))
        return y.reshape(B, L, D)

    def _gn(v, G=32, eps=1e-05):
        B_, C_, H_, W_ = v.shape
        g = v.reshape(B_, G, C_ // G, H_, W_)
        m = jnp.mean(g, axis=(2, 3, 4), keepdims=True)
        s = jnp.var(g, axis=(2, 3, 4), keepdims=True)
        return ((g - m) / jnp.sqrt(s + eps)).reshape(v.shape)

    def _ln_c(v, eps=1e-06):
        m = jnp.mean(v, axis=1, keepdims=True)
        s = jnp.var(v, axis=1, keepdims=True)
        return (v - m) / jnp.sqrt(s + eps)

    def _ln_t(v, eps=1e-05):
        m = jnp.mean(v, axis=-1, keepdims=True)
        s = jnp.var(v, axis=-1, keepdims=True)
        return (v - m) / jnp.sqrt(s + eps)

    def _to_tokens(v):
        B_, C_, H_, W_ = v.shape
        return v.reshape(B_, C_, H_ * W_).transpose(0, 2, 1)

    def _from_tokens(t, like):
        B_, C_, H_, W_ = like.shape
        return t.transpose(0, 2, 1).reshape(B_, C_, H_, W_)
    x = x + _L0_conv_ref(_ln_c(x), L0_conv_norm_w, L0_conv_norm_b, L0_conv_in_proj_w, L0_conv_conv_w, L0_conv_conv_b, L0_conv_x_proj_w, L0_conv_dt_proj_w, L0_conv_dt_proj_b, L0_conv_A_log, L0_conv_D, L0_conv_out_proj_w)
    t = _to_tokens(x)
    t = t + _L0_ffn_ref(_ln_t(t), L0_ffn_gate_w, L0_ffn_w1, L0_ffn_b1, L0_ffn_w2, L0_ffn_b2, L0_ffn_ln_g, L0_ffn_ln_b)
    x = _from_tokens(t, x)
    x = x + _L1_conv_ref(_ln_c(x), L1_conv_A)
    t = _to_tokens(x)
    t = t + _L1_ffn_ref(_ln_t(t), L1_ffn_W_gate, L1_ffn_W1, L1_ffn_W2)
    x = _from_tokens(t, x)
    return x

_drawn_inputs = setup_inputs


def setup_inputs(seed=0):
    import zlib

    import numpy as np

    out = dict(_drawn_inputs(seed))
    spreads = {'L0_conv_norm_w': (1.0, 0.2),
     'L0_conv_norm_b': (0.0, 0.1),
     'L0_conv_conv_b': (0.0, 0.1),
     'L0_conv_dt_proj_b': (-4.600166320800781, 0.6),
     'L0_conv_D': (1.0, 0.2),
     'L0_ffn_b1': (0.0, 0.8),
     'L0_ffn_b2': (0.0, 0.758),
     'L0_ffn_ln_g': (1.0, 0.6),
     'L0_ffn_ln_b': (0.0, 0.8)}
    factors = {'L0_conv_x_proj_w': 29.346,
     'L0_conv_dt_proj_w': 111.204,
     'L0_conv_A_log': 8.0,
     'L0_ffn_gate_w': 5.174,
     'L0_ffn_w1': 8.0,
     'L0_ffn_w2': 8.0,
     'L1_ffn_W_gate': 8.0,
     'L1_ffn_W1': 8.0,
     'L1_ffn_W2': 8.0}
    for name, (base, spread) in spreads.items():
        noise = np.random.default_rng([zlib.crc32(name.encode()), seed]).standard_normal(out[name].shape)
        drawn = base * np.exp(spread * noise) if base else spread * noise
        out[name] = jnp.asarray(drawn.astype(out[name].dtype))
    for name, factor in factors.items():
        out[name] = (out[name] * factor).astype(out[name].dtype)
    return out
```

```python
from contextlib import ExitStack

import numpy as np

import concourse.bass as bass
from concourse import mybir

F32 = mybir.dt.float32
F32R = mybir.dt.float32r
BF16 = mybir.dt.bfloat16
ALU = mybir.AluOpType
ACT = mybir.ActivationFunctionType
AX = mybir.AxisListType

NB = 2
C = 128
H = 16
T = 256
TT = T // 128
DI = 256
DC = DI // 128
NS = 16
TAPS = 4
DTR = 8
BC = 2 * NS
SPLIT = 3
XP = SPLIT * BC + DTR
DT0 = SPLIT * BC
EXPERTS = (8, 16)
UNITS = 16
UW = 256
UC = UW // 128
TOPK = 2
CLAMP = 10.0
RING = 2
ACC = TT * UNITS

COLS = {}
_at = 0
for _name, _width in (("in_w", 2 * DI), ("out_w", DC * C), ("xproj", DC * (DTR + BC)), ("conv_b", DC),
                      ("a_log", DC * NS), ("d_skip", DC), ("norm_w", 1), ("norm_b", 1), ("ln_g", 1),
                      ("ln_b", 1), ("gate0", EXPERTS[0]), ("gate1", EXPERTS[1]), ("b1", UNITS * UC)):
    COLS[_name] = (_at, _at + _width)
    _at += _width
PACKED = _at

SEMS = """
x_loaded params_loaded rows_loaded convw_loaded decay_loaded b2_loaded w1_0_loaded w2_0_loaded
w1_1_loaded w2_1_loaded ident_ready sel_id_ready sel_ready consts_zeroed taps_ready xproj_ready
outw_ready halfb_ready a_exp a_ready diag_ready lag_ready logdecay_ready decay_arg decay_exp decay_ready w1_hi_done
pool_chain dve_chain act_chain
xt_ps x_tok var1 rstd1 var2 rstd2 xs_tok xs_ps xs_ready u_ps z_ps th_u th_z xc_ready sz_ready
xdbl_ps dtr_ready parts_ready dt_ps exp_dt onep_dt ln_dt dt_ready dtx_ready
d_term bc_ready dbx_done cb_done da_done h_done hc_done y_done
yz_ready o_ps var3 rstd3 var4 rstd4 var5 rstd5 xn_tok xn_ps x_full xsplit logit_ps z_sub z_exp comb_ready
comb_ps combT_ready b2_ps
w1_staged h_ready gelu_done w2_done acc_started acc_done
v6 rstd6 lnc_tok lnc_ps lnc_ready mix_ps mix_ready mixT_ps v7 rstd7
out_ps out_sb out_stored
""".split()


def bass_metaformer(nc, x, packed, dt_rows, conv_w, w1_0, w2_0, b2, decay, w1_1, w2_1, out):
    with ExitStack() as ctx:
        def sb(name, shape, dt=F32):
            return ctx.enter_context(nc.sbuf_tensor(name, shape, dt))

        def per_batch(name, shape, dt=F32):
            return [sb(f"{name}_{b}", shape, dt) for b in range(NB)]

        x_cm = sb("x_cm", [C, NB, T])
        par = sb("par", [C, PACKED])
        dtw = sb("dtw", [128, DI])
        convw = sb("convw", [128, TAPS, DI])
        b2_sb = sb("b2_sb", [EXPERTS[0], C])
        decay_sb = sb("decay_sb", [128, H])
        w1 = [sb("w1a", [C, UNITS * UW]), sb("w1b", [C, UNITS * UW])]
        w2 = [sb("w2a", [128, UNITS * UC, C]), sb("w2b", [128, UNITS * UC, C])]

        def col(name):
            return par[:, COLS[name][0]:COLS[name][1]]

        ident = sb("ident", [128, 128])
        sel_id = sb("sel_id", [SPLIT * BC, BC], BF16)
        sel = sb("sel", [SPLIT * BC, BC * 128], BF16)
        neg_half = sb("neg_half", [128, 1])
        euler = sb("euler", [128, 1])
        taps_w = sb("taps_w", [C, TAPS, DI])
        xproj_w = sb("xproj_w", [128, DC, XP])
        outw_half = sb("outw_half", [128, DC * C])
        half_convb = sb("half_convb", [128, DC])
        a_neg = sb("a_neg", [128, DC * NS])
        diag_d = sb("diag_d", [128, DC, 128])
        lag = sb("lag", [128, 128])
        lag_pos = sb("lag_pos", [128, 128])
        causal = sb("causal", [128, 128])
        log_decay = sb("log_decay", [128, H])
        decay_m = sb("decay_m", [128, H, 128])

        x_tok = per_batch("x_tok", [128, TT, C])
        stats = per_batch("stats", [128, TT, 6])
        mv = per_batch("mv", [128, TT, 2])
        veps = per_batch("veps", [128, TT])
        rstd = per_batch("rstd", [128, TT])
        rstd_b = per_batch("rstd_b", [128, TT])
        norm_a = per_batch("norm_a", [128, TT, C])
        norm_b = per_batch("norm_b", [128, TT, C])
        xs_raw = per_batch("xs_raw", [C, T])
        xs = per_batch("xs", [C, TAPS - 1 + T])
        th_u = per_batch("th_u", [128, DC, T])
        th_z = per_batch("th_z", [128, DC, T])
        u_half = per_batch("u_half", [128, DC, T])
        xc = per_batch("xc", [128, DC, T])
        sz = per_batch("sz", [128, DC, T])
        rest = per_batch("rest", [SPLIT * BC, T])
        mid = per_batch("mid", [SPLIT * BC, T], BF16)
        parts = per_batch("parts", [SPLIT * BC, T], BF16)
        dtr = per_batch("dtr", [128, T])
        dt_e = th_u
        dt_w = per_batch("dt_w", [128, DC, T])
        dt_l = u_half
        dt = per_batch("dt", [128, DC, T])
        dtx = per_batch("dtx", [128, DC, T])
        da = [sb(f"da_{p}", [128, DC, T]) for p in range(RING)]
        dbx = [sb(f"dbx_{p}", [128, DC, T]) for p in range(RING)]
        hs = [sb(f"hs_{p}", [128, DC, T]) for p in range(RING)]
        cb = [sb(f"cb_{p}", [128, T]) for p in range(RING)]
        hc = [sb(f"hc_{p}", [128, DC, T]) for p in range(RING)]
        yz = dtx

        t_tok = per_batch("t_tok", [128, TT, C])
        xn_tok = per_batch("xn_tok", [128, TT, C])
        xg_tok = per_batch("xg_tok", [128, TT, C])
        x_full = per_batch("x_full", [C, T])
        x_hi = per_batch("x_hi", [C, T], F32R)
        x_lo = per_batch("x_lo", [C, T], F32R)
        mx = per_batch("mx", [128, TT])
        z_sub = [[sb(f"z_sub_{l}_{b}", [128, TT, EXPERTS[l]]) for b in range(NB)] for l in range(2)]
        z_exp = [[sb(f"z_exp_{l}_{b}", [128, TT, EXPERTS[l]]) for b in range(NB)] for l in range(2)]
        prob = [[sb(f"prob_{l}_{b}", [128, TT, EXPERTS[l] + 8]) for b in range(NB)] for l in range(2)]
        left = [[sb(f"left_{l}_{b}", [128, TT, EXPERTS[l] + 8]) for b in range(NB)] for l in range(2)]
        top8 = per_batch("top8", [128, TT, 8])
        top2 = per_batch("top2", [128, TT, 8])
        zsum = per_batch("zsum", [128, TT])
        comb8 = per_batch("comb8", [128, TT, EXPERTS[0]])
        comb = [[sb(f"comb_{l}_{b}", [128, TT, UNITS]) for b in range(NB)] for l in range(2)]
        combT = per_batch("combT", [EXPERTS[0], T])
        w1_hi = [sb(f"w1_hi_{p}", [C, UW], F32R) for p in range(RING)]
        w1_lo = [sb(f"w1_lo_{p}", [C, UW], F32R) for p in range(RING)]
        hid = [sb(f"hid_{p}", [128, UC, T]) for p in range(RING)]
        acc = [sb(f"acc_{k}", [128, TT, C]) for k in range(2 * NB)]
        lnc = per_batch("lnc", [C, T])
        mix = per_batch("mix", [C, T])
        out_sb = per_batch("out_sb", [C, T])

        b_ps = [ctx.enter_context(nc.psum_tensor(f"b_ps_{p}", [128, 2, T], F32)) for p in range(RING)]
        y_ps = ctx.enter_context(nc.psum_tensor("y_ps", [128, DC, T], F32))
        m_ps = ctx.enter_context(nc.psum_tensor("m_ps", [128, 512], F32))
        h_ps = [ctx.enter_context(nc.psum_tensor(f"h_ps_{p}", [128, UC, T], F32)) for p in range(RING)]
        o_ps = [ctx.enter_context(nc.psum_tensor(f"o_ps_{p}", [128, 2, T], F32)) for p in range(RING)]
        xt_ps = [m_ps[:, 0:T].rearrange("p (t c) -> p t c", t=TT), y_ps[:, 0, :].rearrange("p (t c) -> p t c", t=TT)]
        xs_ps = [m_ps[:, T:2 * T], y_ps[:, 1, :]]
        u_ps = [h_ps[0], o_ps[0]]
        z_ps = [h_ps[1], o_ps[1]]
        xd_ps = [b_ps[0][:, 0, :], b_ps[1][:, 0, :]]
        bc_ps = [(b_ps[p][:, 0, :], h_ps[p][:, 0, :]) for p in range(RING)]
        dt_ps = [h_ps[0], o_ps[0]]
        m_tok = m_ps[:, 0:T].rearrange("p (t c) -> p t c", t=TT)

        s = {name: ctx.enter_context(nc.semaphore(name)) for name in SEMS}
        block = ctx.enter_context(nc.Block())

        def cut(layer, b, steps):
            plan, u = [], 0
            for step in steps:
                plan += [("experts", layer, b, u, u + 2), step]
                u += 2
            return plan + [("experts", layer, b, u, UNITS)]

        plan = [("project", 0), ("project", 1), ("step_size", 0), ("step_size", 1),
                ("scan", 0), ("gate_out", 0), ("norm_out", 0), ("moe_in", 0, 0), ("route", 0, 0), ("bias2", 0),
                ("scan", 1), ("gate_out", 1)]
        plan += cut(0, 0, [("norm_out", 1), ("moe_in", 0, 1), ("route", 0, 1), ("bias2", 1)])
        plan += cut(0, 1, [("mix_norm", 0), ("mix", 0), ("mix_back", 0), ("moe_in", 1, 0), ("route", 1, 0)])
        plan += cut(1, 0, [("mix_norm", 1), ("mix", 1), ("mix_back", 1), ("moe_in", 1, 1), ("route", 1, 1)])
        plan += cut(1, 1, [("store", 0)]) + [("store", 1)]

        @block.sync
        def _(sp):
            sp.dma_start(x_cm[:], x).then_inc(s["x_loaded"], 16)
            sp.dma_start(par[:], packed).then_inc(s["params_loaded"], 16)
            sp.dma_start(convw[:], conv_w).then_inc(s["convw_loaded"], 16)
            sp.dma_start(dtw[DT0:DT0 + DTR + 1, :], dt_rows).then_inc(s["rows_loaded"], 16)
            sp.dma_start(decay_sb[:], decay).then_inc(s["decay_loaded"], 16)
            sp.dma_start(b2_sb[:], b2).then_inc(s["b2_loaded"], 16)
            for layer, (w1_d, w2_d) in enumerate(((w1_0, w2_0), (w1_1, w2_1))):
                n = EXPERTS[layer] // 2
                fw = UNITS * UW // EXPERTS[layer]
                w1_v = w1[layer][:].rearrange("c (e f) -> c e f", f=fw)
                for i in range(2):
                    sp.dma_start(w1_v[:, n * i:n * (i + 1), :],
                                 w1_d[n * i:n * (i + 1)].rearrange("e c f -> c e f")).then_inc(s[f"w1_{layer}_loaded"], 16)
                    m = UNITS * UC // 2
                    sp.dma_start(w2[layer][:, m * i:m * (i + 1), :],
                                 w2_d.rearrange("e (j p) c -> p (e j) c", p=128)[:, m * i:m * (i + 1), :]
                                 ).then_inc(s[f"w2_{layer}_loaded"], 16)
            for b in range(NB):
                sp.wait_ge(s["out_sb"], b + 1)
                sp.dma_start(out[:, b, :], out_sb[b][:]).then_inc(s["out_stored"], 16)
            sp.wait_ge(s["out_stored"], 16 * NB)

        @block.gpsimd
        def _(pool):
            chain = [0]

            def link(ins):
                chain[0] += 1
                ins.then_inc(s["pool_chain"], 1)
                pool.wait_ge(s["pool_chain"], chain[0])

            def power(dst, base, exponent, done):
                n = 1
                for d in dst.shape[1:]:
                    n *= d
                nc.gpsimd.tensor_tensor(dst, base, exponent, ALU.pow).then_inc(done, 1)

            def half(shape):
                return neg_half[:, 0:1].to_broadcast(shape)

            pool.sem_inc(s["hc_done"], RING)
            link(nc.gpsimd.memset(ident[:], 0.0))
            nc.gpsimd.affine_select(out=ident[:], in_=ident[:], compare_op=ALU.not_equal, fill=1.0, base=0,
                                    pattern=[[-1, 128]], channel_multiplier=1).then_inc(s["ident_ready"], 1)
            link(nc.gpsimd.memset(neg_half[:], -0.5))
            link(nc.gpsimd.memset(euler[:], float(np.exp(1.0))))
            for b in range(NB):
                link(nc.gpsimd.memset(xs[b][:, 0:TAPS - 1], 0.0))
                link(nc.gpsimd.memset(dtr[b][DT0:DT0 + 32, :], 1.0))
                link(nc.gpsimd.memset(da[b][:, :, 0:1], 0.0))
                link(nc.gpsimd.memset(top2[b][:], -1.0))
                for layer in range(2):
                    link(nc.gpsimd.memset(prob[layer][b][:], -1.0))
            link(nc.gpsimd.memset(sel_id[:], 0.0))
            for j in range(SPLIT):
                link(nc.gpsimd.affine_select(out=sel_id[:], in_=sel_id[:], compare_op=ALU.not_equal, fill=1.0,
                                             base=-BC * j, pattern=[[-1, BC]], channel_multiplier=1))
            pool.sem_inc(s["sel_id_ready"], 1)
            pool.wait_ge(s["params_loaded"], 16)
            pool.wait_ge(s["convw_loaded"], 16)
            nc.gpsimd.tensor_tensor(taps_w[:], convw[:],
                                    col("in_w")[:, 0:DI].rearrange("c (o d) -> c o d", o=1).to_broadcast([C, TAPS, DI]),
                                    ALU.mult).then_inc(s["taps_ready"], 1)

            def scan(b):
                with pool.Fori(0, NS // RING) as i:
                    for p in range(RING):
                        m = i * RING + (NS * b + p)
                        pool.wait_ge(s["h_done"], m + 1 + RING)
                        pool.wait_ge(s["cb_done"], m + 1 + RING)
                        pool.wait_ge(s["y_done"], m + 1)
                        nc.gpsimd.tensor_tensor(hc[p][:], hs[p][:],
                                                cb[p][:].rearrange("p (o t) -> p o t", o=1).to_broadcast([128, DC, T]),
                                                ALU.mult).then_inc(s["hc_done"], 1)

            def experts(layer, b, u0, u1):
                k = NB * layer + b

                def unit(u, p):
                    pool.wait_ge(s["h_ready"], u + (UNITS * k + 1))
                    w = w1[layer][:, bass.ds(u * UW, UW)]
                    pool.wait_ge(s[f"w1_{layer}_loaded"], 32)
                    nc.gpsimd.tensor_copy(w1_hi[p][:], w).then_inc(s["w1_hi_done"], 1)
                    pool.wait_ge(s[f"w1_{layer}_loaded"], 32)
                    pool.wait_ge(s["w1_hi_done"], u + (UNITS * k + 1))
                    nc.gpsimd.tensor_tensor(w1_lo[p][:], w, w1_hi[p][:].bitcast(F32), ALU.subtract).then_inc(s["w1_staged"], 1)

                repeat(pool, u0 + RING if u0 else 0, min(u1 + RING, UNITS), unit)

            def rsqrt(b, dst, var_sem, done, k):
                pool.wait_ge(s[var_sem], k + 1)
                power(dst, veps[b][:], half([128, TT]), s[done])

            for step, *arg in plan:
                if step == "project":
                    b, = arg
                    rsqrt(b, rstd[b][:], "var1", "rstd1", b)
                    rsqrt(b, rstd[b][:], "var2", "rstd2", b)
                    if b == 0:
                        link(nc.gpsimd.iota(lag[:], pattern=[[1, 128]], base=0, channel_multiplier=-1,
                                            allow_small_or_imprecise_dtypes=True))
                        link(nc.gpsimd.tensor_scalar(lag_pos[:], lag[:], 0.0, None, ALU.max))
                        link(nc.gpsimd.tensor_scalar(causal[:], lag[:], 0.0, None, ALU.is_ge))
                        nc.gpsimd.tensor_scalar(outw_half[:], col("out_w"), 0.5, None, ALU.mult).then_inc(s["outw_ready"], 1)
                elif step == "step_size" and arg[0] == 0:
                    pool.wait_ge(s["a_exp"], 1)
                    nc.gpsimd.tensor_scalar(a_neg[:], a_neg[:], -1.0, None, ALU.mult).then_inc(s["a_ready"], 1)
                elif step == "step_size":
                    pool.wait_ge(s["logdecay_ready"], 1)
                    for r in range(H):
                        ins = nc.gpsimd.tensor_scalar(decay_m[:, r, :], lag_pos[:], log_decay[:, r:r + 1], None, ALU.mult)
                    ins.then_inc(s["decay_arg"], 1)
                elif step == "scan":
                    scan(*arg)
                    if arg[0] == 0:
                        pool.wait_ge(s["decay_exp"], 1)
                        nc.gpsimd.tensor_tensor(decay_m[:], decay_m[:],
                                                causal[:].rearrange("p (o t) -> p o t", o=1).to_broadcast([128, H, 128]),
                                                ALU.mult).then_inc(s["decay_ready"], 1)
                elif step == "norm_out":
                    b, = arg
                    rsqrt(b, rstd[b][:], "var3", "rstd3", b)
                    rsqrt(b, rstd[b][:], "var4", "rstd4", b)
                    rsqrt(b, rstd_b[b][:], "var5", "rstd5", b)
                elif step == "mix_norm":
                    rsqrt(arg[0], rstd[arg[0]][:], "v6", "rstd6", arg[0])
                elif step == "mix_back":
                    rsqrt(arg[0], rstd[arg[0]][:], "v7", "rstd7", arg[0])
                elif step == "route":
                    layer, b = arg
                    k = NB * layer + b
                    pool.wait_ge(s["z_sub"], k + 1)
                    power(z_exp[layer][b][:], euler[:, 0:1].to_broadcast([128, TT * EXPERTS[layer]]).rearrange("p (t e) -> p t e", t=TT),
                          z_sub[layer][b][:], s["z_exp"])
                elif step == "experts":
                    experts(*arg)

        @block.scalar
        def _(act):
            chain = [0]

            def link(ins):
                chain[0] += 1
                ins.then_inc(s["act_chain"], 1)
                act.wait_ge(s["act_chain"], chain[0])

            act.sem_inc(s["cb_done"], RING)
            act.sem_inc(s["gelu_done"], RING)
            act.wait_ge(s["sel_id_ready"], 1)
            nc.scalar.activation(sel[:].rearrange("k (n m) -> k n m", m=128),
                                 sel_id[:].rearrange("k (n o) -> k n o", o=1).to_broadcast([SPLIT * BC, BC, 128]),
                                 ACT.Copy).then_inc(s["sel_ready"], 1)
            act.wait_ge(s["params_loaded"], 16)
            nc.scalar.activation(half_convb[:], col("conv_b"), ACT.Copy, scale=0.5).then_inc(s["halfb_ready"], 1)

            def project(b):
                act.wait_ge(s["halfb_ready"], 1)
                act.wait_ge(s["u_ps"], b + 1)
                for c in range(DC):
                    ins = nc.scalar.activation(u_half[b][:, c, :], u_ps[b][:, c, :], ACT.Identity,
                                               bias=half_convb[:, c:c + 1], scale=0.5)
                link(ins)
                nc.scalar.activation(th_u[b][:], u_half[b][:], ACT.Tanh).then_inc(s["th_u"], 1)
                act.wait_ge(s["z_ps"], b + 1)
                nc.scalar.activation(th_z[b][:], z_ps[b][:], ACT.Tanh, scale=0.5).then_inc(s["th_z"], 1)

            def step_size(b):
                if b == 0:
                    nc.scalar.activation(a_neg[:], col("a_log"), ACT.Exp).then_inc(s["a_exp"], 1)
                act.wait_ge(s["dt_ps"], b + 1)
                link(nc.scalar.activation(dt_w[b][:], dt_ps[b][:], ACT.Abs))
                nc.scalar.activation(dt_e[b][:], dt_w[b][:], ACT.Exp, scale=-1.0).then_inc(s["exp_dt"], 1)
                act.wait_ge(s["onep_dt"], b + 1)
                nc.scalar.activation(dt_l[b][:], dt_w[b][:], ACT.Ln).then_inc(s["ln_dt"], 1)
                if b == 0:
                    act.wait_ge(s["lag_ready"], 1)
                    nc.scalar.activation(log_decay[:], decay_sb[:], ACT.Ln).then_inc(s["logdecay_ready"], 1)
                else:
                    act.wait_ge(s["decay_arg"], 1)
                    nc.scalar.activation(decay_m[:], decay_m[:], ACT.Exp).then_inc(s["decay_exp"], 1)

            def scan(b):
                act.wait_ge(s["a_ready"], 1)
                act.wait_ge(s["dt_ready"], b + 1)
                with act.Fori(0, NS // RING) as i:
                    for p in range(RING):
                        m = i * RING + (NS * b + p)
                        act.wait_ge(s["h_done"], m + 1)
                        for c in range(DC):
                            ins = nc.scalar.activation(da[p][:, c, 1:T], dt[b][:, c, 1:T], ACT.Exp,
                                                       scale=a_neg[:, bass.ds(i * RING + (c * NS + p), 1)])
                        ins.then_inc(s["da_done"], 1)
                        act.wait_ge(s["bc_ready"], m + 1)
                        act.wait_ge(s["hc_done"], m + 1)
                        nc.scalar.activation(cb[p][:], bc_ps[p][1], ACT.Copy).then_inc(s["cb_done"], 1)

            def experts(layer, b, u0, u1):
                k = NB * layer + b

                def unit(u, p):
                    act.wait_ge(s["h_ready"], u + (UNITS * k + 1 + RING))
                    act.wait_ge(s["w2_done"], u + (UNITS * k + 1))
                    if layer == 0:
                        for c in range(UC):
                            at = COLS["b1"][0] + c
                            ins = nc.scalar.activation(hid[p][:, c, :], h_ps[p][:, c, :], ACT.Gelu,
                                                       bias=par[:, bass.ds(u * UC + at, 1)])
                    else:
                        ins = nc.scalar.activation(hid[p][:], h_ps[p][:], ACT.Gelu)
                    ins.then_inc(s["gelu_done"], 1)

                repeat(act, u0, u1, unit)

            for step, *arg in plan:
                if step == "project":
                    project(*arg)
                elif step == "step_size":
                    step_size(*arg)
                elif step == "scan":
                    scan(*arg)
                elif step == "experts":
                    experts(*arg)

        @block.vector
        def _(dve):
            chain = [0]

            def link(ins):
                chain[0] += 1
                ins.then_inc(s["dve_chain"], 1)
                dve.wait_ge(s["dve_chain"], chain[0])

            dve.sem_inc(s["dbx_done"], RING)
            dve.sem_inc(s["h_done"], RING)
            dve.sem_inc(s["acc_done"], RING * TT)

            def statistics(b, src, eps, done):
                for t in range(TT):
                    ins = nc.vector.bn_stats(stats[b][:, t, :], src[:, t, :])
                link(ins)
                for t in range(TT):
                    ins = nc.vector.bn_aggr(mv[b][:, t, :], stats[b][:, t, :])
                link(ins)
                nc.vector.tensor_scalar(veps[b][:], mv[b][:, :, 1], eps, None, ALU.add).then_inc(s[done], 1)

            def normalise(b, dst, src, root, rstd_sem, k):
                dve.wait_ge(s[rstd_sem], k + 1)
                for t in range(TT):
                    ins = nc.vector.tensor_scalar(dst[:, t, :], src[:, t, :], mv[b][:, t, 0:1], root[:, t:t + 1],
                                                  ALU.subtract, ALU.mult)
                return ins

            def clamp(dst, src):
                return nc.vector.tensor_scalar(dst, src, CLAMP, -CLAMP, ALU.min, ALU.max)

            def prepare():
                dve.wait_ge(s["params_loaded"], 16)
                wx = col("xproj").rearrange("p (c r) -> p c r", c=DC)
                for j in range(SPLIT):
                    nc.vector.tensor_copy(xproj_w[:, :, BC * j:BC * (j + 1)], wx[:, :, DTR:DTR + BC])
                nc.vector.tensor_copy(xproj_w[:, :, DT0:XP], wx[:, :, 0:DTR]).then_inc(s["xproj_ready"], 1)
                dve.wait_ge(s["ident_ready"], 1)
                for c in range(DC):
                    ins = nc.vector.tensor_scalar(diag_d[:, c, :], ident[:], col("d_skip")[:, c:c + 1], None, ALU.mult)
                ins.then_inc(s["diag_ready"], 1)
                dve.wait_ge(s["decay_loaded"], 16)
                nc.vector.tensor_scalar(decay_sb[:], decay_sb[:], 1e-6, None, ALU.max).then_inc(s["lag_ready"], 1)

            def project(b):
                dve.wait_ge(s["xt_ps"], b + 1)
                link(nc.vector.tensor_copy(x_tok[b][:], xt_ps[b]))
                statistics(b, x_tok[b], 1e-6, "var1")
                link(normalise(b, norm_a[b], x_tok[b], rstd[b], "rstd1", b))
                link(clamp(norm_a[b][:], norm_a[b][:]))
                statistics(b, norm_a[b], 1e-5, "var2")
                normalise(b, norm_b[b], norm_a[b], rstd[b], "rstd2", b).then_inc(s["xs_tok"], 1)
                if b == 0:
                    prepare()
                dve.wait_ge(s["xs_ps"], b + 1)
                link(nc.vector.tensor_scalar(xs_raw[b][:], xs_ps[b], col("norm_w"), col("norm_b"), ALU.mult, ALU.add))
                clamp(xs[b][:, TAPS - 1:TAPS - 1 + T], xs_raw[b][:]).then_inc(s["xs_ready"], 1)
                dve.wait_ge(s["th_u"], b + 1)
                nc.vector.scalar_tensor_tensor(xc[b][:], th_u[b][:], 1.0, u_half[b][:], ALU.add, ALU.mult).then_inc(s["xc_ready"], 1)
                dve.wait_ge(s["th_z"], b + 1)
                nc.vector.scalar_tensor_tensor(sz[b][:], th_z[b][:], 1.0, z_ps[b][:], ALU.add, ALU.mult).then_inc(s["sz_ready"], 1)

            def step_size(b):
                dve.wait_ge(s["xdbl_ps"], b + 1)
                nc.vector.tensor_copy(dtr[b][DT0:XP, :], xd_ps[b][DT0:XP, :]).then_inc(s["dtr_ready"], 1)
                n = SPLIT * BC
                link(nc.vector.tensor_copy(parts[b][:], xd_ps[b][0:n, :]))
                link(nc.vector.tensor_tensor(rest[b][:], xd_ps[b][0:n, :], parts[b][:], ALU.subtract))
                link(nc.vector.tensor_copy(mid[b][:], rest[b][:]))
                nc.vector.tensor_copy(parts[b][BC:2 * BC, :], mid[b][BC:2 * BC, :])
                nc.vector.tensor_tensor(parts[b][2 * BC:n, :], rest[b][2 * BC:n, :], mid[b][2 * BC:n, :],
                                        ALU.subtract).then_inc(s["parts_ready"], 1)
                dve.wait_ge(s["exp_dt"], b + 1)
                nc.vector.tensor_scalar(dt_w[b][:], dt_e[b][:], 1.0, None, ALU.add).then_inc(s["onep_dt"], 1)
                dve.wait_ge(s["onep_dt"], b + 1)
                link(nc.vector.scalar_tensor_tensor(dt_e[b][:], dt_w[b][:], -1.0, dt_e[b][:], ALU.add, ALU.subtract))
                dve.wait_ge(s["ln_dt"], b + 1)
                link(nc.vector.tensor_tensor(dt_l[b][:], dt_l[b][:], dt_e[b][:], ALU.subtract))
                nc.vector.scalar_tensor_tensor(dt[b][:], dt_ps[b][:], 0.0, dt_l[b][:], ALU.max, ALU.add).then_inc(s["dt_ready"], 1)
                dve.wait_ge(s["dt_ready"], b + 1)
                link(nc.vector.tensor_tensor(dtx[b][:], dt[b][:], xc[b][:], ALU.mult))

            def scan(b):
                def input_n(n, p):
                    m = n + NS * b
                    dve.wait_ge(s["h_done"], m + 1)
                    dve.wait_ge(s["bc_ready"], m + 1)
                    nc.vector.tensor_tensor(dbx[p][:], dtx[b][:], bc_ps[p][0].rearrange("p (o t) -> p o t", o=1).to_broadcast([128, DC, T]),
                                            ALU.mult).then_inc(s["dbx_done"], 1)

                def scan_n(n, p):
                    m = n + NS * b
                    dve.wait_ge(s["dbx_done"], m + 1 + RING)
                    dve.wait_ge(s["da_done"], m + 1)
                    dve.wait_ge(s["hc_done"], m + 1)
                    nc.vector.tensor_tensor_scan(hs[p][:].rearrange("p c t -> p (c t)"),
                                                 da[p][:].rearrange("p c t -> p (c t)"),
                                                 dbx[p][:].rearrange("p c t -> p (c t)"),
                                                 0.0, ALU.mult, ALU.add).then_inc(s["h_done"], 1)

                input_n(0, 0)
                with dve.Fori(0, NS // RING - 1) as i:
                    for p in range(RING):
                        input_n(i * RING + (p + 1), 1 - p)
                        scan_n(i * RING + p, p)
                input_n(NS - 1, 1)
                scan_n(NS - 2, 0)
                scan_n(NS - 1, 1)

            def gate_out(b):
                dve.wait_ge(s["y_done"], NS * (b + 1) + RING)
                nc.vector.tensor_tensor(yz[b][:], y_ps[:], sz[b][:], ALU.mult).then_inc(s["yz_ready"], 1)

            def norm_out(b):
                dve.wait_ge(s["o_ps"], b + 1)
                link(clamp(norm_a[b][:], m_tok))
                statistics(b, norm_a[b], 1e-5, "var3")
                link(normalise(b, norm_b[b], norm_a[b], rstd[b], "rstd3", b))
                link(clamp(norm_b[b][:], norm_b[b][:]))
                link(nc.vector.tensor_tensor(t_tok[b][:], x_tok[b][:], norm_b[b][:], ALU.add))
                statistics(b, t_tok[b], 1e-5, "var4")
                link(normalise(b, xn_tok[b], t_tok[b], rstd[b], "rstd4", b))
                link(nc.vector.tensor_tensor(veps[b][:], rstd[b][:], rstd[b][:], ALU.mult))
                link(nc.vector.tensor_tensor(veps[b][:], veps[b][:], mv[b][:, :, 1], ALU.mult))
                nc.vector.tensor_scalar(veps[b][:], veps[b][:], 1e-5, None, ALU.add).then_inc(s["var5"], 1)
                link(nc.vector.tensor_tensor(t_tok[b][:], t_tok[b][:], xn_tok[b][:], ALU.add))
                dve.wait_ge(s["rstd5"], b + 1)
                for t in range(TT):
                    ins = nc.vector.tensor_scalar(xg_tok[b][:, t, :], xn_tok[b][:, t, :], rstd_b[b][:, t:t + 1], None, ALU.mult)
                ins.then_inc(s["xn_tok"], 1)

            def moe_in(layer, b):
                k = NB * layer + b
                dve.wait_ge(s["xn_ps"], k + 1)
                if layer == 0:
                    link(nc.vector.tensor_scalar(x_full[b][:], m_ps[:, 0:T], col("ln_g"), col("ln_b"), ALU.mult, ALU.add))
                else:
                    link(nc.vector.tensor_copy(x_full[b][:], m_ps[:, 0:T]))
                dve.sem_inc(s["x_full"], 1)
                link(nc.vector.tensor_copy(x_hi[b][:], x_full[b][:]))
                nc.vector.tensor_tensor(x_lo[b][:], x_full[b][:], x_hi[b][:].bitcast(F32), ALU.subtract).then_inc(s["xsplit"], 1)

            def route(layer, b):
                k, n = NB * layer + b, EXPERTS[layer]
                wide = [128, TT, n]
                pr, rest_p = prob[layer][b], left[layer][b]
                logits = m_ps[:, 0:TT * n].rearrange("p (t e) -> p t e", t=TT)
                dve.wait_ge(s["logit_ps"], k + 1)
                link(nc.vector.tensor_reduce(out=mx[b][:], in_=logits, op=ALU.max, axis=AX.X))
                nc.vector.tensor_tensor(z_sub[layer][b][:], logits,
                                        mx[b][:].rearrange("p (t o) -> p t o", o=1).to_broadcast(wide),
                                        ALU.subtract).then_inc(s["z_sub"], 1)
                dve.wait_ge(s["z_exp"], k + 1)
                link(nc.vector.tensor_reduce(out=zsum[b][:], in_=z_exp[layer][b][:], op=ALU.add, axis=AX.X))
                link(nc.vector.reciprocal(zsum[b][:], zsum[b][:]))
                link(nc.vector.tensor_tensor(pr[:, :, 0:n], z_exp[layer][b][:],
                                             zsum[b][:].rearrange("p (t o) -> p t o", o=1).to_broadcast(wide), ALU.mult))
                for t in range(TT):
                    ins = nc.vector.max(top8[b][:, t, :], pr[:, t, :])
                link(ins)
                link(nc.vector.tensor_copy(top2[b][:, :, 0:TOPK], top8[b][:, :, 0:TOPK]))
                for t in range(TT):
                    ins = nc.vector.match_replace(out=rest_p[:, t, :], in_to_replace=top2[b][:, t, :],
                                                  in_values=pr[:, t, :], imm_value=0.0)
                link(ins)
                if layer == 0:
                    link(nc.vector.tensor_tensor(comb8[b][:], pr[:, :, 0:n], rest_p[:, :, 0:n], ALU.subtract))
                    nc.vector.tensor_copy(comb[0][b][:].rearrange("p t (e o) -> p t e o", o=UNITS // n),
                                          comb8[b][:].rearrange("p t (e o) -> p t e o", o=1).to_broadcast([128, TT, n, UNITS // n])
                                          ).then_inc(s["comb_ready"], 1)
                else:
                    nc.vector.tensor_tensor(comb[1][b][:], pr[:, :, 0:n], rest_p[:, :, 0:n], ALU.subtract).then_inc(s["comb_ready"], 1)

            def bias2(b):
                dve.wait_ge(s["comb_ps"], b + 1)
                nc.vector.tensor_copy(combT[b][:], m_ps[0:EXPERTS[0], 0:T]).then_inc(s["combT_ready"], 1)
                dve.wait_ge(s["b2_ps"], b + 1)
                nc.vector.tensor_tensor(acc[b][:], t_tok[b][:], m_tok, ALU.add).then_inc(s["acc_started"], 1)

            def experts(layer, b, u0, u1):
                k = NB * layer + b

                def unit(u, p):
                    dve.wait_ge(s["w2_done"], u + (UNITS * k + 1 + RING))
                    for t in range(TT):
                        dve.wait_ge(s["acc_done"], u * TT + (ACC * k + TT + t + 1))
                        nc.vector.scalar_tensor_tensor(acc[k][:, t, :], o_ps[p][:, 0, 128 * t:128 * (t + 1)],
                                                       comb[layer][b][:, t, bass.ds(u, 1)], acc[k][:, t, :],
                                                       ALU.mult, ALU.add).then_inc(s["acc_done"], 1)

                if u0 == 0:
                    dve.wait_ge(s["comb_ready"], k + 1)
                    dve.wait_ge(s["acc_started"], k + 1)
                repeat(dve, u0, u1, unit)

            def mix_norm(b):
                dve.wait_ge(s["acc_done"], ACC * (b + 1) + RING * TT)
                statistics(b, acc[b], 1e-6, "v6")
                normalise(b, norm_a[b], acc[b], rstd[b], "rstd6", b).then_inc(s["lnc_tok"], 1)

            def mix_dve(b):
                dve.wait_ge(s["lnc_ps"], b + 1)
                nc.vector.tensor_copy(lnc[b][:], m_ps[:, 0:T]).then_inc(s["lnc_ready"], 1)
                dve.wait_ge(s["mix_ps"], b + 1)
                nc.vector.tensor_copy(mix[b][:], m_ps[:, T:2 * T]).then_inc(s["mix_ready"], 1)

            def mix_back(b):
                k = NB + b
                dve.wait_ge(s["mixT_ps"], b + 1)
                nc.vector.tensor_tensor(acc[k][:], acc[b][:], m_tok, ALU.add).then_inc(s["acc_started"], 1)
                dve.wait_ge(s["acc_started"], k + 1)
                statistics(b, acc[k], 1e-5, "v7")
                normalise(b, xg_tok[b], acc[k], rstd[b], "rstd7", b).then_inc(s["xn_tok"], 1)

            def store(b):
                dve.wait_ge(s["out_ps"], b + 1)
                nc.vector.tensor_copy(out_sb[b][:], m_ps[:, 0:T]).then_inc(s["out_sb"], 1)

            does = {"project": project, "step_size": step_size, "scan": scan, "gate_out": gate_out, "norm_out": norm_out,
                    "moe_in": moe_in, "route": route, "bias2": bias2, "experts": experts, "mix_norm": mix_norm,
                    "mix": mix_dve, "mix_back": mix_back, "store": store}
            for step, *arg in plan:
                does[step](*arg)

        @block.tensor
        def _(pe):
            pe.sem_inc(s["h_ready"], RING)
            pe.sem_inc(s["w2_done"], RING)
            pe.sem_inc(s["y_done"], RING)

            def to_channels(dst, src):
                for t in range(TT):
                    ins = nc.tensor.transpose(dst[:, 128 * t:128 * (t + 1)], src[:, t, :], ident[:])
                return ins

            def to_tokens(dst, src):
                for t in range(TT):
                    ins = nc.tensor.transpose(dst[:, t, :], src[:, 128 * t:128 * (t + 1)], ident[:])
                return ins

            def project(b):
                pe.wait_ge(s["ident_ready"], 1)
                pe.wait_ge(s["x_loaded"], 16)
                to_tokens(xt_ps[b], x_cm[:, b, :]).then_inc(s["xt_ps"], 1)
                pe.wait_ge(s["xs_tok"], b + 1)
                to_channels(xs_ps[b], norm_b[b]).then_inc(s["xs_ps"], 1)
                pe.wait_ge(s["taps_ready"], 1)
                pe.wait_ge(s["xs_ready"], b + 1)
                for c in range(DC):
                    for k in range(TAPS):
                        ins = nc.tensor.matmul(u_ps[b][:, c, :], taps_w[:, k, 128 * c:128 * (c + 1)], xs[b][:, k:k + T],
                                               start=(k == 0), stop=(k == TAPS - 1))
                ins.then_inc(s["u_ps"], 1)
                for c in range(DC):
                    ins = nc.tensor.matmul(z_ps[b][:, c, :], col("in_w")[:, DI + 128 * c:DI + 128 * (c + 1)],
                                           xs[b][:, TAPS - 1:TAPS - 1 + T], start=True, stop=True)
                ins.then_inc(s["z_ps"], 1)

            def step_size(b):
                pe.wait_ge(s["xproj_ready"], 1)
                pe.wait_ge(s["xc_ready"], b + 1)
                for c in range(DC):
                    ins = nc.tensor.matmul(xd_ps[b][0:XP, :], xproj_w[:, c, :], xc[b][:, c, :], start=(c == 0), stop=(c == DC - 1))
                ins.then_inc(s["xdbl_ps"], 1)
                pe.wait_ge(s["rows_loaded"], 16)
                pe.wait_ge(s["dtr_ready"], b + 1)
                for c in range(DC):
                    ins = nc.tensor.matmul(dt_ps[b][:, c, :], dtw[DT0:XP + 1, 128 * c:128 * (c + 1)], dtr[b][DT0:XP + 1, :],
                                           start=True, stop=True)
                ins.then_inc(s["dt_ps"], 1)

            def scan(b):
                def spread(n, p):
                    m = n + NS * b
                    pe.wait_ge(s["dbx_done"], m + 1)
                    pe.wait_ge(s["cb_done"], m + 1)
                    for i in range(2):
                        ins = nc.tensor.matmul(bc_ps[p][i], sel[:, bass.ds((n + NS * i) * 128, 128)], parts[b][:],
                                               start=True, stop=True)
                    ins.then_inc(s["bc_ready"], 1)

                def add(n, p, last=False):
                    pe.wait_ge(s["hc_done"], n + (NS * b + 1 + RING))
                    nc.tensor.matmul(y_ps[:], ident[:], hc[p][:], start=False, stop=last).then_inc(s["y_done"], 1)

                pe.wait_ge(s["sel_ready"], 1)
                pe.wait_ge(s["parts_ready"], NB)
                pe.wait_ge(s["dt_ready"], b + 1)
                spread(0, 0)
                spread(1, 1)
                pe.wait_ge(s["diag_ready"], 1)
                pe.wait_ge(s["xs_ready"], NB)
                if b:
                    pe.wait_ge(s["yz_ready"], b)
                for c in range(DC):
                    nc.tensor.matmul(y_ps[:, c, :], diag_d[:, c, :], xc[b][:, c, :], start=(c == 0), stop=False)
                with pe.Fori(0, NS // RING - 1) as i:
                    for p in range(RING):
                        spread(i * RING + (p + RING), p)
                        add(i * RING + p, p)
                add(NS - 2, 0)
                add(NS - 1, 1, last=True)

            def norm_out(b):
                pe.wait_ge(s["outw_ready"], 1)
                pe.wait_ge(s["yz_ready"], b + 1)
                for t in range(TT):
                    for c in range(DC):
                        ins = nc.tensor.matmul(m_tok[:, t, :], yz[b][:, c, 128 * t:128 * (t + 1)],
                                               outw_half[:, 128 * c:128 * (c + 1)], start=(c == 0), stop=(c == DC - 1))
                ins.then_inc(s["o_ps"], 1)

            def moe_in(layer, b):
                pe.wait_ge(s["xn_tok"], NB * layer + b + 1)
                to_channels(m_ps[:, 0:T], xg_tok[b]).then_inc(s["xn_ps"], 1)

            def route(layer, b):
                n = EXPERTS[layer]
                pe.wait_ge(s["x_full"], NB * layer + b + 1)
                for t in range(TT):
                    ins = nc.tensor.matmul(m_ps[:, n * t:n * (t + 1)], x_full[b][:, 128 * t:128 * (t + 1)], col(f"gate{layer}"),
                                           start=True, stop=True)
                ins.then_inc(s["logit_ps"], 1)

            def bias2(b):
                pe.wait_ge(s["comb_ready"], b + 1)
                for t in range(TT):
                    ins = nc.tensor.transpose(m_ps[0:EXPERTS[0], 128 * t:128 * (t + 1)], comb8[b][:, t, :], ident[:])
                ins.then_inc(s["comb_ps"], 1)
                pe.wait_ge(s["b2_loaded"], 16)
                pe.wait_ge(s["combT_ready"], b + 1)
                for t in range(TT):
                    ins = nc.tensor.matmul(m_tok[:, t, :], combT[b][:, 128 * t:128 * (t + 1)], b2_sb[:], start=True, stop=True)
                ins.then_inc(s["b2_ps"], 1)

            def experts(layer, b, u0, u1):
                k = NB * layer + b

                def hidden(u, p):
                    pe.wait_ge(s["w1_staged"], u + (UNITS * k + 1))
                    pe.wait_ge(s["gelu_done"], u + (UNITS * k + 1))
                    for c in range(UC):
                        at = slice(128 * c, 128 * (c + 1))
                        nc.tensor.matmul(h_ps[p][:, c, :], w1_hi[p][:, at], x_hi[b][:], start=True, stop=False)
                        nc.tensor.matmul(h_ps[p][:, c, :], w1_hi[p][:, at], x_lo[b][:], start=False, stop=False)
                        ins = nc.tensor.matmul(h_ps[p][:, c, :], w1_lo[p][:, at], x_hi[b][:], start=False, stop=True)
                    ins.then_inc(s["h_ready"], 1)

                def output(u, p):
                    pe.wait_ge(s["gelu_done"], u + (UNITS * k + 1 + RING))
                    pe.wait_ge(s["acc_done"], u * TT + (ACC * k + TT))
                    for t in range(TT):
                        for c in range(UC):
                            ins = nc.tensor.matmul(o_ps[p][:, 0, 128 * t:128 * (t + 1)], hid[p][:, c, 128 * t:128 * (t + 1)],
                                                   w2[layer][:, bass.ds(u * UC + c, 1), :], start=(c == 0), stop=(c == UC - 1))
                    ins.then_inc(s["w2_done"], 1)

                def unit(u, p):
                    hidden(u + 1, 1 - p)
                    output(u, p)

                if u0 == 0:
                    pe.wait_ge(s["xsplit"], k + 1)
                    if b == 0:
                        pe.wait_ge(s[f"w2_{layer}_loaded"], 32)
                    hidden(0, 0)
                if u1 == UNITS:
                    repeat(pe, u0, u1 - RING, unit)
                    hidden(UNITS - 1, 1)
                    output(UNITS - 2, 0)
                    output(UNITS - 1, 1)
                else:
                    repeat(pe, u0, u1, unit)

            def mix_pe(b):
                pe.wait_ge(s["lnc_tok"], b + 1)
                to_channels(m_ps[:, 0:T], norm_a[b]).then_inc(s["lnc_ps"], 1)
                pe.wait_ge(s["decay_ready"], 1)
                pe.wait_ge(s["lnc_ready"], b + 1)
                w = T // H
                for r in range(H):
                    ins = nc.tensor.matmul(m_ps[:, T + w * r:T + w * (r + 1)], decay_m[:, r, :], lnc[b][:, w * r:w * (r + 1)],
                                           start=True, stop=True)
                ins.then_inc(s["mix_ps"], 1)

            def mix_back(b):
                pe.wait_ge(s["mix_ready"], b + 1)
                to_tokens(m_tok, mix[b]).then_inc(s["mixT_ps"], 1)

            def store(b):
                pe.wait_ge(s["acc_done"], ACC * (NB + b + 1) + RING * TT)
                to_channels(m_ps[:, 0:T], acc[NB + b]).then_inc(s["out_ps"], 1)

            does = {"project": project, "step_size": step_size, "scan": scan, "norm_out": norm_out, "moe_in": moe_in,
                    "route": route, "bias2": bias2, "experts": experts, "mix": mix_pe, "mix_back": mix_back, "store": store}
            for step, *arg in plan:
                if step in does:
                    does[step](*arg)


def repeat(engine, first, end, unit):
    if end - first <= RING:
        for u in range(first, end):
            unit(u, u % RING)
        return
    with engine.Fori(0, (end - first) // RING) as i:
        for p in range(RING):
            unit(i * RING + (first + p), p)


def kernel(x, L0_conv_norm_w, L0_conv_norm_b, L0_conv_in_proj_w, L0_conv_conv_w, L0_conv_conv_b, L0_conv_x_proj_w,
           L0_conv_dt_proj_w, L0_conv_dt_proj_b, L0_conv_A_log, L0_conv_D, L0_conv_out_proj_w, L0_ffn_gate_w,
           L0_ffn_w1, L0_ffn_b1, L0_ffn_w2, L0_ffn_b2, L0_ffn_ln_g, L0_ffn_ln_b, L1_conv_A, L1_ffn_W_gate,
           L1_ffn_W1, L1_ffn_W2):
    import concourse.bacc as bacc
    from concourse.bass_utils import run_bass_kernel_spmd

    def chunks(a):
        a = np.asarray(a).reshape(-1, 128, np.asarray(a).size // np.asarray(a).shape[0])
        return a.transpose(1, 0, 2).reshape(128, -1)

    parts = {"in_w": np.asarray(L0_conv_in_proj_w).T, "out_w": chunks(np.asarray(L0_conv_out_proj_w).T),
             "xproj": chunks(np.asarray(L0_conv_x_proj_w).T), "conv_b": chunks(L0_conv_conv_b),
             "a_log": chunks(L0_conv_A_log), "d_skip": chunks(L0_conv_D), "norm_w": chunks(L0_conv_norm_w),
             "norm_b": chunks(L0_conv_norm_b), "ln_g": chunks(L0_ffn_ln_g), "ln_b": chunks(L0_ffn_ln_b),
             "gate0": np.asarray(L0_ffn_gate_w), "gate1": np.asarray(L1_ffn_W_gate),
             "b1": chunks(np.asarray(L0_ffn_b1).reshape(-1))}
    arrays = {
        "x_in": np.asarray(x).reshape(NB, C, T),
        "packed_in": np.concatenate([parts[name] for name in COLS], axis=1),
        "dt_rows_in": np.concatenate([np.asarray(L0_conv_dt_proj_w).T, np.asarray(L0_conv_dt_proj_b).reshape(1, DI)]),
        "conv_w_in": np.asarray(L0_conv_conv_w).reshape(DI, TAPS).T.reshape(1, TAPS * DI),
        "w1_0_in": np.asarray(L0_ffn_w1), "w2_0_in": np.asarray(L0_ffn_w2), "b2_in": np.asarray(L0_ffn_b2),
        "decay_in": np.asarray(L1_conv_A).reshape(1, H),
        "w1_1_in": np.asarray(L1_ffn_W1), "w2_1_in": np.asarray(L1_ffn_W2),
    }
    arrays = {name: np.ascontiguousarray(a) for name, a in arrays.items()}
    nc = bacc.Bacc("TRN2", target_bir_lowering=False, num_devices=1)
    ap = {name: nc.dram_tensor(name, a.shape, mybir.dt.from_np(a.dtype), kind="ExternalInput").ap()
          for name, a in arrays.items()}
    y = nc.dram_tensor("y_out", (NB, C, T), F32, kind="ExternalOutput").ap()
    bass_metaformer(nc, ap["x_in"].rearrange("b c t -> c b t"), ap["packed_in"], ap["dt_rows_in"],
                    ap["conv_w_in"].rearrange("o (k d) -> o k d", k=TAPS).to_broadcast([128, TAPS, DI]),
                    ap["w1_0_in"], ap["w2_0_in"], ap["b2_in"], ap["decay_in"].to_broadcast([128, H]),
                    ap["w1_1_in"], ap["w2_1_in"], y.rearrange("b c t -> c b t"))
    r = run_bass_kernel_spmd(nc, [arrays], core_ids=[0])
    return r.results[0]["y_out"].reshape(NB, C, H, T // H)
```

```python
from contextlib import ExitStack

import numpy as np

import concourse.bass as bass
from concourse import mybir

F32 = mybir.dt.float32
F32R = mybir.dt.float32r
BF16 = mybir.dt.bfloat16
ALU = mybir.AluOpType
ACT = mybir.ActivationFunctionType
AX = mybir.AxisListType

NB = 2
C = 128
H = 16
T = 256
TT = T // 128
DI = 256
DC = DI // 128
NS = 16
TAPS = 4
DTR = 8
BC = 2 * NS
SPLIT = 3
XP = SPLIT * BC + DTR
DT0 = SPLIT * BC
EXPERTS = (8, 16)
UNITS = 16
UW = 256
UC = UW // 128
TOPK = 2
CLAMP = 10.0
RING = 2
PAIR = 2
NP = NS // PAIR
ACC = TT * UNITS

COLS = {}
_at = 0
for _name, _width in (("in_w", 2 * DI), ("out_w", DC * C), ("xproj", DC * (DTR + BC)), ("conv_b", DC), ("conv_w", DC * TAPS),
                      ("a_log", DC * NS), ("d_skip", DC), ("norm_w", 1), ("norm_b", 1), ("ln_g", 1),
                      ("ln_b", 1), ("gate0", EXPERTS[0]), ("gate1", EXPERTS[1]), ("b1", UNITS * UC)):
    COLS[_name] = (_at, _at + _width)
    _at += _width
PACKED = _at

SEMS = """
x_loaded params_loaded rows_loaded decay_loaded b2_loaded w1_0_loaded w2_0_loaded w1_1_loaded w2_1_loaded
ident_ready sel_id_ready sel_ready xproj_ready outw_ready a_exp a_ready diag_ready
decay_clipped logdecay_ready decay_arg decay_exp decay_ready
pool_chain dve_chain act_chain
xt_ps var1 rstd1 var2 rstd2 xs_tok xs_ps xs_ready xin_ps z_ps u_ready th_u th_z xc_ready sz_ready
xdbl_ps dtr_ready parts_ready dt_ps exp_dt onep_dt ln_dt dt_ready
bc_ready dbx_done cb_done da_done h_done hc_done y_done
yz_ready o_ps var3 rstd3 var4 rstd4 var5 rstd5 xn_tok xn_ps x_full xsplit logit_ps z_sub z_tanh comb_ready
comb_ps combT_ready b2_ps
w1_hi_done w1_staged h_ready gelu_done w2_done acc_started acc_done
var6 rstd6 lnc_tok lnc_ps lnc_ready mix_ps mix_ready mixT_ps var7 rstd7
out_ps out_sb out_stored
""".split()


def bass_metaformer(nc, x, packed, dt_rows, w1_0, w2_0, b2, decay, w1_1, w2_1, out):
    with ExitStack() as ctx:
        def sb(name, shape, dt=F32):
            return ctx.enter_context(nc.sbuf_tensor(name, shape, dt))

        def per_batch(name, shape, dt=F32):
            return [sb(f"{name}_{b}", shape, dt) for b in range(NB)]

        x_cm = sb("x_cm", [C, NB, T])
        par = sb("par", [C, PACKED])
        dtw = sb("dtw", [128, DI])
        b2_sb = sb("b2_sb", [EXPERTS[0], C])
        decay_sb = sb("decay_sb", [128, H])
        w1 = [sb("w1a", [C, UNITS * UW]), sb("w1b", [C, UNITS * UW])]
        w2 = [sb("w2a", [128, UNITS * UC, C]), sb("w2b", [128, UNITS * UC, C])]

        def col(name):
            return par[:, COLS[name][0]:COLS[name][1]]

        ident = sb("ident", [128, 128])
        sel_id = sb("sel_id", [SPLIT * BC, BC], BF16)
        sel = sb("sel", [SPLIT * BC, BC * 128], BF16)
        neg_half = sb("neg_half", [128, 1])
        one = sb("one", [128, 1])
        xproj_w = sb("xproj_w", [128, DC, XP])
        outw_half = sb("outw_half", [128, DC * C])
        a_neg = sb("a_neg", [128, DC * NS])
        diag_d = sb("diag_d", [128, DC, 128])
        lag = sb("lag", [128, 128])
        lag_pos = sb("lag_pos", [128, 128])
        log_decay = sb("log_decay", [128, H])
        decay_m = sb("decay_m", [128, H, 128])

        x_tok = sb("x_tok", [128, NB * TT, C])
        xs_a = sb("xs_a", [128, NB * TT, C])
        xs_b = sb("xs_b", [128, NB * TT, C])
        stats4 = sb("stats4", [128, NB * TT, 6])
        mv4 = sb("mv4", [128, NB * TT, 2])
        veps4 = sb("veps4", [128, NB * TT])
        rstd4 = sb("rstd4", [128, NB * TT])
        xs = sb("xs", [C, NB, T])
        u2 = sb("u2", [128, DC, NB, T])
        th_u = sb("th_u", [128, DC, NB, T])
        th_z = sb("th_z", [128, DC, NB, T])
        xc2 = sb("xc2", [128, DC, NB, T])
        sz2 = sb("sz2", [128, DC, NB, T])
        rest = xs_a[0:SPLIT * BC].rearrange("p (b t) c -> p b (t c)", b=NB)
        mid = sb("mid", [SPLIT * BC, NB, T], BF16)
        parts = sb("parts", [SPLIT * BC, NB, T], BF16)
        dtr = sb("dtr", [128, NB, T])
        dt_e = th_u
        dt_l = u2
        dt_w = th_z
        dt = sb("dt", [128, DC, NB, T])
        dtx = per_batch("dtx", [128, DC, T])
        da = [sb(f"da_{p}", [128, PAIR, DC, T]) for p in range(RING)]
        dbx = [sb(f"dbx_{p}", [128, PAIR, DC, T]) for p in range(RING)]
        hs = [sb(f"hs_{p}", [128, PAIR, DC, T]) for p in range(RING)]
        cb = [sb(f"cb_{p}", [128, PAIR, T]) for p in range(RING)]
        hc = [sb(f"hc_{p}", [128, PAIR, DC, T]) for p in range(RING)]
        yz = dtx

        stats = per_batch("stats", [128, TT, 6])
        mv = per_batch("mv", [128, TT, 2])
        veps = per_batch("veps", [128, TT])
        rstd = per_batch("rstd", [128, TT])
        rstd_b = per_batch("rstd_b", [128, TT])
        norm_a = per_batch("norm_a", [128, TT, C])
        norm_b = per_batch("norm_b", [128, TT, C])
        t_tok = per_batch("t_tok", [128, TT, C])
        xn_tok = per_batch("xn_tok", [128, TT, C])
        xg_tok = per_batch("xg_tok", [128, TT, C])
        x_full = per_batch("x_full", [C, T])
        x_hi = per_batch("x_hi", [C, T], F32R)
        x_lo = per_batch("x_lo", [C, T], F32R)
        mx = per_batch("mx", [128, TT])
        z_sub = [[sb(f"z_sub_{l}_{b}", [128, TT, EXPERTS[l]]) for b in range(NB)] for l in range(2)]
        z_den = [[sb(f"z_den_{l}_{b}", [128, TT, EXPERTS[l]]) for b in range(NB)] for l in range(2)]
        z_exp = [[sb(f"z_exp_{l}_{b}", [128, TT, EXPERTS[l]]) for b in range(NB)] for l in range(2)]
        prob = [[sb(f"prob_{l}_{b}", [128, TT, EXPERTS[l] + 8]) for b in range(NB)] for l in range(2)]
        left = [[sb(f"left_{l}_{b}", [128, TT, EXPERTS[l] + 8]) for b in range(NB)] for l in range(2)]
        top8 = per_batch("top8", [128, TT, 8])
        top2 = per_batch("top2", [128, TT, 8])
        zsum = per_batch("zsum", [128, TT])
        comb8 = per_batch("comb8", [128, TT, EXPERTS[0]])
        comb = [[sb(f"comb_{l}_{b}", [128, TT, UNITS]) for b in range(NB)] for l in range(2)]
        combT = per_batch("combT", [EXPERTS[0], T])
        w1_hi = [sb(f"w1_hi_{p}", [C, UW], F32R) for p in range(RING)]
        w1_lo = [sb(f"w1_lo_{p}", [C, UW], F32R) for p in range(RING)]
        hid = [sb(f"hid_{p}", [128, UC, T]) for p in range(RING)]
        acc = [sb(f"acc_{k}", [128, TT, C]) for k in range(2 * NB)]
        lnc = per_batch("lnc", [C, T])
        mix = [a[:].rearrange("p t c -> p (t c)") for a in norm_b]
        out_sb = lnc

        def banks(name, n):
            return ctx.enter_context(nc.psum_tensor(name, [128, n, 512], F32))

        b_ps, h_ps, o_ps = banks("b_ps", RING), banks("h_ps", RING), banks("o_ps", RING)
        y_ps, m_ps = banks("y_ps", 1)[:, 0, :], banks("m_ps", 1)[:, 0, :]
        m_tok = m_ps[:, 0:T].rearrange("p (t c) -> p t c", t=TT)
        y_sum = y_ps.rearrange("p (c t) -> p c t", c=DC)

        def by_batch(bank):
            return bank.rearrange("p (b t) -> p b t", b=NB)

        xt_ps, xs_ps = m_ps, y_ps
        xin_ps, z_ps, dt_ps, xd_ps = h_ps, o_ps, h_ps, b_ps[:, 0, :]
        bc_ps = [(b_ps[:, p, :], o_ps[:, p, :]) for p in range(RING)]

        def dt_view(b):
            return dt_ps[:, :, T * b:T * (b + 1)]

        s = {name: ctx.enter_context(nc.semaphore(name)) for name in SEMS}
        block = ctx.enter_context(nc.Block())

        finish = ["gate_out", "out_proj", "out_norm", "skip_norm", "inner_norm", "inner_scale", "to_channel", "expert_in",
                  "logits", "logit_max", "softmax", "top2", "gates_t", "gates_tc", "bias2", "start_sum"]
        mixer = ["mix_stats", "mix_norm", "mix_t", "mix_tc", "mix", "mix_c", "mix_back", "mix_add",
                 "inner_scale", "to_channel", "expert_in", "logits", "logit_max", "softmax", "top2"]

        def between(work, end, steps, layer, b, apart):
            plan, k = [], 0
            while steps:
                if k < end:
                    plan.append((*work, k, k + 1))
                    k += 1
                plan += [(name, layer, b) for name in steps[:apart]]
                steps = steps[apart:]
            if k % RING and k < end:
                plan.append((*work, k, k + 1))
                k += 1
            return plan + ([(*work, k, end)] if k < end else [])

        plan = [("project",), ("x_proj",), ("step_size",), ("scan", 0, 0, NP)]
        plan += between(("scan", 1), NP, finish, 0, 0, 2)
        plan += between(("experts", 0, 0), UNITS, finish, 0, 1, 1)
        plan += between(("experts", 0, 1), UNITS, mixer, 1, 0, 1)
        plan += between(("experts", 1, 0), UNITS, mixer, 1, 1, 1)
        plan += between(("experts", 1, 1), UNITS, ["store_t", "store"], 1, 0, 1)
        plan += [("store_t", 1, 1), ("store", 1, 1)]

        @block.sync
        def _(sp):
            sp.dma_start(x_cm[:], x).then_inc(s["x_loaded"], 16)
            sp.dma_start(par[:], packed).then_inc(s["params_loaded"], 16)
            sp.dma_start(dtw[DT0:DT0 + DTR + 1, :], dt_rows).then_inc(s["rows_loaded"], 16)
            sp.dma_start(decay_sb[:], decay).then_inc(s["decay_loaded"], 16)
            sp.dma_start(b2_sb[:], b2).then_inc(s["b2_loaded"], 16)
            for layer, (w1_d, w2_d) in enumerate(((w1_0, w2_0), (w1_1, w2_1))):
                n = EXPERTS[layer] // 2
                fw = UNITS * UW // EXPERTS[layer]
                w1_v = w1[layer][:].rearrange("c (e f) -> c e f", f=fw)
                for i in range(2):
                    sp.dma_start(w1_v[:, n * i:n * (i + 1), :],
                                 w1_d[n * i:n * (i + 1)].rearrange("e c f -> c e f")).then_inc(s[f"w1_{layer}_loaded"], 16)
                    m = UNITS * UC // 2
                    sp.dma_start(w2[layer][:, m * i:m * (i + 1), :],
                                 w2_d.rearrange("e (j p) c -> p (e j) c", p=128)[:, m * i:m * (i + 1), :]
                                 ).then_inc(s[f"w2_{layer}_loaded"], 16)
            for b in range(NB):
                sp.wait_ge(s["out_sb"], b + 1)
                sp.dma_start(out[:, b, :], out_sb[b][:]).then_inc(s["out_stored"], 16)
            sp.wait_ge(s["out_stored"], 16 * NB)

        @block.gpsimd
        def _(pool):
            chain = [0]

            def link(ins):
                chain[0] += 1
                ins.then_inc(s["pool_chain"], 1)
                pool.wait_ge(s["pool_chain"], chain[0])

            def rsqrt(dst, var, var_sem, done, k):
                pool.wait_ge(s[var_sem], k + 1)
                nc.gpsimd.tensor_tensor(dst, var, neg_half[:, 0:1].to_broadcast(list(var.shape)), ALU.pow).then_inc(s[done], 1)

            pool.sem_inc(s["hc_done"], RING)
            link(nc.gpsimd.memset(ident[:], 0.0))
            nc.gpsimd.affine_select(out=ident[:], in_=ident[:], compare_op=ALU.not_equal, fill=1.0, base=0,
                                    pattern=[[-1, 128]], channel_multiplier=1).then_inc(s["ident_ready"], 1)
            link(nc.gpsimd.memset(neg_half[:], -0.5))
            link(nc.gpsimd.memset(one[:], 1.0))
            link(nc.gpsimd.memset(sel_id[:], 0.0))
            for j in range(SPLIT):
                link(nc.gpsimd.affine_select(out=sel_id[:], in_=sel_id[:], compare_op=ALU.not_equal, fill=1.0,
                                             base=-BC * j, pattern=[[-1, BC]], channel_multiplier=1))
            pool.sem_inc(s["sel_id_ready"], 1)
            link(nc.gpsimd.iota(lag[:], pattern=[[1, 128]], base=0, channel_multiplier=-1,
                                allow_small_or_imprecise_dtypes=True))
            link(nc.gpsimd.tensor_scalar(lag_pos[:], lag[:], 0.0, None, ALU.max))
            link(nc.gpsimd.tensor_scalar(lag[:], lag[:], 0.0, None, ALU.is_ge))
            link(nc.gpsimd.memset(dtr[DT0:DT0 + 32, :, :], 1.0))
            for b in range(NB):
                link(nc.gpsimd.memset(da[b][:, :, :, 0:1], 0.0))
                link(nc.gpsimd.memset(top2[b][:], -1.0))
                for layer in range(2):
                    link(nc.gpsimd.memset(prob[layer][b][:], -1.0))

            def project():
                rsqrt(rstd4[:], veps4[:], "var1", "rstd1", 0)
                rsqrt(rstd4[:], veps4[:], "var2", "rstd2", 0)
                pool.wait_ge(s["params_loaded"], 16)
                nc.gpsimd.tensor_scalar(outw_half[:], col("out_w"), 0.5, None, ALU.mult).then_inc(s["outw_ready"], 1)
                pool.wait_ge(s["logdecay_ready"], 1)
                for r in range(H):
                    ins = nc.gpsimd.tensor_scalar(decay_m[:, r, :], lag_pos[:], log_decay[:, r:r + 1], None, ALU.mult)
                ins.then_inc(s["decay_arg"], 1)
                pool.wait_ge(s["a_exp"], 1)
                nc.gpsimd.tensor_scalar(a_neg[:], a_neg[:], -1.0, None, ALU.mult).then_inc(s["a_ready"], 1)
                pool.wait_ge(s["decay_exp"], 1)
                nc.gpsimd.tensor_tensor(decay_m[:], decay_m[:],
                                        lag[:].rearrange("p (o t) -> p o t", o=1).to_broadcast([128, H, 128]),
                                        ALU.mult).then_inc(s["decay_ready"], 1)

            def scan(b, k0, k1):
                def pair(k, p):
                    m = k + NP * b
                    pool.wait_ge(s["h_done"], m + (1 + RING))
                    pool.wait_ge(s["cb_done"], m + (1 + RING))
                    pool.wait_ge(s["y_done"], m + 1)
                    for i in range(PAIR):
                        ins = nc.gpsimd.tensor_tensor(
                            hc[p][:, i], hs[p][:, i], cb[p][:, i:i + 1, :].to_broadcast([128, DC, T]), ALU.mult)
                    ins.then_inc(s["hc_done"], 1)

                repeat(pool, k0, k1, pair)

            def experts(layer, b, u0, u1):
                k = NB * layer + b

                def unit(u, p):
                    pool.wait_ge(s["h_ready"], u + (UNITS * k + 1))
                    w = w1[layer][:, bass.ds(u * UW, UW)]
                    pool.wait_ge(s[f"w1_{layer}_loaded"], 32)
                    nc.gpsimd.tensor_tensor(w1_hi[p][:], w, one[:, 0:1].to_broadcast([C, UW]), ALU.mult).then_inc(s["w1_hi_done"], 1)
                    pool.wait_ge(s[f"w1_{layer}_loaded"], 32)
                    pool.wait_ge(s["w1_hi_done"], u + (UNITS * k + 1))
                    nc.gpsimd.tensor_tensor(w1_lo[p][:], w, w1_hi[p][:].bitcast(F32), ALU.subtract).then_inc(s["w1_staged"], 1)

                repeat(pool, u0 + RING if u0 else 0, min(u1 + RING, UNITS), unit)

            roots = {"out_norm": ("var3", "rstd3"), "skip_norm": ("var4", "rstd4"), "mix_stats": ("var6", "rstd6"),
                     "mix_add": ("var7", "rstd7")}
            for step, *arg in plan:
                if step == "project":
                    project()
                elif step == "scan":
                    scan(*arg)
                elif step == "experts":
                    experts(*arg)
                elif step in roots:
                    b = arg[1]
                    rsqrt(rstd[b][:], veps[b][:], *roots[step], b)
                elif step == "inner_norm":
                    b = arg[1]
                    rsqrt(rstd_b[b][:], veps[b][:], "var5", "rstd5", b)

        @block.scalar
        def _(act):
            chain = [0]

            def link(ins):
                chain[0] += 1
                ins.then_inc(s["act_chain"], 1)
                act.wait_ge(s["act_chain"], chain[0])

            act.sem_inc(s["cb_done"], RING)
            act.sem_inc(s["gelu_done"], RING)

            def project():
                act.wait_ge(s["decay_clipped"], 1)
                nc.scalar.activation(log_decay[:], decay_sb[:], ACT.Ln).then_inc(s["logdecay_ready"], 1)
                act.wait_ge(s["params_loaded"], 16)
                nc.scalar.activation(a_neg[:], col("a_log"), ACT.Exp).then_inc(s["a_exp"], 1)
                act.wait_ge(s["sel_id_ready"], 1)
                nc.scalar.activation(sel[:].rearrange("k (n m) -> k n m", m=128),
                                     sel_id[:].rearrange("k (n o) -> k n o", o=1).to_broadcast([SPLIT * BC, BC, 128]),
                                     ACT.Copy).then_inc(s["sel_ready"], 1)
                act.wait_ge(s["decay_arg"], 1)
                nc.scalar.activation(decay_m[:], decay_m[:], ACT.Exp).then_inc(s["decay_exp"], 1)
                for c in range(DC):
                    act.wait_ge(s["u_ready"], c + 1)
                    nc.scalar.activation(th_u[:, c], u2[:, c], ACT.Tanh, scale=0.5).then_inc(s["th_u"], 1)
                act.wait_ge(s["z_ps"], 1)
                for c in range(DC):
                    nc.scalar.activation(th_z[:, c], by_batch(z_ps[:, c, :]), ACT.Tanh, scale=0.5).then_inc(s["th_z"], 1)

            def step_size():
                act.wait_ge(s["sz_ready"], 1)
                act.wait_ge(s["dt_ps"], 1)
                link(nc.scalar.activation(dt_w[:].rearrange("p c b t -> p c (b t)"), dt_ps[:], ACT.Abs))
                for b in range(NB):
                    nc.scalar.activation(dt_e[:, :, b, :], dt_w[:, :, b, :], ACT.Exp, scale=-1.0).then_inc(s["exp_dt"], 1)
                for b in range(NB):
                    act.wait_ge(s["onep_dt"], b + 1)
                    nc.scalar.activation(dt_l[:, :, b, :], dt_w[:, :, b, :], ACT.Ln).then_inc(s["ln_dt"], 1)

            def scan(b, k0, k1):
                def pair(k, p):
                    m = k + NP * b
                    act.wait_ge(s["h_done"], m + 1)
                    for i in range(PAIR):
                        for c in range(DC):
                            ins = nc.scalar.activation(da[p][:, i, c, 1:T], dt[:, c, b, 1:T], ACT.Exp,
                                                       scale=a_neg[:, bass.ds(k * PAIR + (c * NS + i), 1)])
                    ins.then_inc(s["da_done"], 1)
                    act.wait_ge(s["bc_ready"], m + 1)
                    act.wait_ge(s["hc_done"], m + 1)
                    nc.scalar.activation(cb[p][:], bc_ps[p][1].rearrange("p (i t) -> p i t", i=PAIR),
                                         ACT.Copy).then_inc(s["cb_done"], 1)

                if k0 == 0:
                    act.wait_ge(s["a_ready"], 1)
                    act.wait_ge(s["dt_ready"], b + 1)
                repeat(act, k0, k1, pair)

            def softmax(layer, b):
                act.wait_ge(s["z_sub"], NB * layer + b + 1)
                nc.scalar.activation(z_exp[layer][b][:], z_sub[layer][b][:], ACT.Tanh, scale=0.25).then_inc(s["z_tanh"], 1)

            def experts(layer, b, u0, u1):
                k = NB * layer + b

                def unit(u, p):
                    act.wait_ge(s["h_ready"], u + (UNITS * k + 1 + RING))
                    act.wait_ge(s["w2_done"], u + (UNITS * k + 1))
                    if layer == 0:
                        for c in range(UC):
                            at = COLS["b1"][0] + c
                            ins = nc.scalar.activation(hid[p][:, c, :], h_ps[:, p, T * c:T * (c + 1)], ACT.Gelu,
                                                       bias=par[:, bass.ds(u * UC + at, 1)])
                    else:
                        ins = nc.scalar.activation(hid[p][:], h_ps[:, p, :].rearrange("p (c t) -> p c t", c=UC), ACT.Gelu)
                    ins.then_inc(s["gelu_done"], 1)

                repeat(act, u0, u1, unit)

            does = {"project": project, "step_size": step_size, "scan": scan, "logit_max": softmax, "experts": experts}
            for step, *arg in plan:
                if step in does:
                    does[step](*arg)

        @block.vector
        def _(dve):
            chain = [0]

            def link(ins):
                chain[0] += 1
                ins.then_inc(s["dve_chain"], 1)
                dve.wait_ge(s["dve_chain"], chain[0])

            dve.sem_inc(s["dbx_done"], RING)
            dve.sem_inc(s["h_done"], RING)
            dve.sem_inc(s["acc_done"], RING * TT)

            def statistics(n, src, stats, mv, veps, eps, done):
                for t in range(n):
                    ins = nc.vector.bn_stats(stats[:, t, :], src[:, t, :])
                link(ins)
                for t in range(n):
                    ins = nc.vector.bn_aggr(mv[:, t, :], stats[:, t, :])
                link(ins)
                nc.vector.tensor_scalar(veps[:], mv[:, :, 1], eps, None, ALU.add).then_inc(s[done], 1)

            def batch_statistics(b, src, eps, done):
                statistics(TT, src, stats[b], mv[b], veps[b], eps, done)

            def normalise(n, dst, src, mv, root, root_sem, k):
                dve.wait_ge(s[root_sem], k + 1)
                for t in range(n):
                    ins = nc.vector.tensor_scalar(dst[:, t, :], src[:, t, :], mv[:, t, 0:1], root[:, t:t + 1],
                                                  ALU.subtract, ALU.mult)
                return ins

            def clamp(dst, src):
                return nc.vector.tensor_scalar(dst, src, CLAMP, -CLAMP, ALU.min, ALU.max)

            def prepare():
                dve.wait_ge(s["decay_loaded"], 16)
                nc.vector.tensor_scalar(decay_sb[:], decay_sb[:], 1e-6, None, ALU.max).then_inc(s["decay_clipped"], 1)
                dve.wait_ge(s["params_loaded"], 16)
                wx = col("xproj").rearrange("p (c r) -> p c r", c=DC)
                for j in range(SPLIT):
                    nc.vector.tensor_scalar(xproj_w[:, :, BC * j:BC * (j + 1)], wx[:, :, DTR:DTR + BC], 0.5, None, ALU.mult)
                nc.vector.tensor_scalar(xproj_w[:, :, DT0:XP], wx[:, :, 0:DTR], 0.5, None, ALU.mult).then_inc(s["xproj_ready"], 1)
                dve.wait_ge(s["ident_ready"], 1)
                for c in range(DC):
                    ins = nc.vector.tensor_scalar(diag_d[:, c, :], ident[:], col("d_skip")[:, c:c + 1], 0.5, ALU.mult, ALU.mult)
                ins.then_inc(s["diag_ready"], 1)

            def project():
                n = NB * TT
                dve.wait_ge(s["xt_ps"], 1)
                link(nc.vector.tensor_copy(x_tok[:], xt_ps.rearrange("p (t c) -> p t c", t=n)))
                statistics(n, x_tok, stats4, mv4, veps4, 1e-6, "var1")
                prepare()
                link(normalise(n, xs_a, x_tok, mv4, rstd4, "rstd1", 0))
                link(clamp(xs_a[:], xs_a[:]))
                statistics(n, xs_a, stats4, mv4, veps4, 1e-5, "var2")
                normalise(n, xs_b, xs_a, mv4, rstd4, "rstd2", 0).then_inc(s["xs_tok"], 1)
                dve.wait_ge(s["xs_ps"], 1)
                link(nc.vector.tensor_scalar(xs[:], by_batch(xs_ps), col("norm_w"), col("norm_b"), ALU.mult, ALU.add))
                clamp(xs[:], xs[:]).then_inc(s["xs_ready"], 1)
                taps = col("conv_w").rearrange("p (c k) -> p c k", c=DC)
                last = [0] * DC
                for back in range(TAPS):
                    for c in range(DC):
                        x_c, w = by_batch(xin_ps[:, c, :]), taps[:, c, TAPS - 1 - back:TAPS - back]
                        if back == 0:
                            dve.wait_ge(s["xin_ps"], c + 1)
                            ins = nc.vector.tensor_scalar(u2[:, c], x_c, w, col("conv_b")[:, c:c + 1], ALU.mult, ALU.add)
                        else:
                            dve.wait_ge(s["dve_chain"], last[c])
                            ins = nc.vector.scalar_tensor_tensor(u2[:, c, :, back:T], x_c[:, :, 0:T - back], w,
                                                                 u2[:, c, :, back:T], ALU.mult, ALU.add)
                        if back < TAPS - 1:
                            chain[0] += 1
                            last[c] = chain[0]
                            ins.then_inc(s["dve_chain"], 1)
                        else:
                            ins.then_inc(s["u_ready"], 1)
                for c in range(DC):
                    dve.wait_ge(s["th_u"], c + 1)
                    dve.wait_ge(s["u_ready"], c + 1)
                    nc.vector.scalar_tensor_tensor(xc2[:, c], th_u[:, c], 1.0, u2[:, c], ALU.add, ALU.mult).then_inc(s["xc_ready"], 1)
                for c in range(DC):
                    dve.wait_ge(s["th_z"], c + 1)
                    ins = nc.vector.scalar_tensor_tensor(sz2[:, c], th_z[:, c], 1.0, by_batch(z_ps[:, c, :]), ALU.add, ALU.mult)
                ins.then_inc(s["sz_ready"], 1)

            def x_proj():
                dve.wait_ge(s["xdbl_ps"], 1)
                rows = by_batch(xd_ps)
                nc.vector.tensor_copy(dtr[DT0:XP], rows[DT0:XP]).then_inc(s["dtr_ready"], 1)
                n = SPLIT * BC
                link(nc.vector.tensor_copy(parts[:], rows[0:n]))
                link(nc.vector.tensor_tensor(rest, rows[0:n], parts[:], ALU.subtract))
                link(nc.vector.tensor_copy(mid[:], rest))
                nc.vector.tensor_copy(parts[BC:2 * BC], mid[BC:2 * BC])
                nc.vector.tensor_tensor(parts[2 * BC:n], rest[2 * BC:n], mid[2 * BC:n], ALU.subtract).then_inc(s["parts_ready"], 1)

            def step_size():
                w, e, ln = ([a[:, :, b, :] for b in range(NB)] for a in (dt_w, dt_e, dt_l))
                for b in range(NB):
                    dve.wait_ge(s["exp_dt"], b + 1)
                    nc.vector.tensor_scalar(w[b], e[b], 1.0, None, ALU.add).then_inc(s["onep_dt"], 1)
                    dve.wait_ge(s["onep_dt"], b + 1)
                    link(nc.vector.scalar_tensor_tensor(e[b], w[b], -1.0, e[b], ALU.add, ALU.subtract))
                for b in range(NB):
                    dve.wait_ge(s["ln_dt"], b + 1)
                    link(nc.vector.tensor_tensor(ln[b], ln[b], e[b], ALU.subtract))
                    nc.vector.scalar_tensor_tensor(dt[:, :, b, :], dt_view(b), 0.0, ln[b], ALU.max, ALU.add).then_inc(s["dt_ready"], 1)
                    dve.wait_ge(s["dt_ready"], b + 1)
                    link(nc.vector.scalar_tensor_tensor(dtx[b][:], xc2[:, :, b, :], 0.5, dt[:, :, b, :], ALU.mult, ALU.mult))

            def scan(b, k0, k1):
                def inputs(k, p):
                    m = k + NP * b
                    dve.wait_ge(s["h_done"], m + 1)
                    dve.wait_ge(s["bc_ready"], m + 1)
                    rows = bc_ps[p][0].rearrange("p (i o t) -> p i o t", i=PAIR, o=1)
                    nc.vector.tensor_tensor(dbx[p][:], dtx[b][:].rearrange("p (o c) t -> p o c t", o=1).to_broadcast([128, PAIR, DC, T]),
                                            rows.to_broadcast([128, PAIR, DC, T]), ALU.mult).then_inc(s["dbx_done"], 1)

                def states(k, p):
                    m = k + NP * b
                    dve.wait_ge(s["dbx_done"], m + (1 + RING))
                    dve.wait_ge(s["da_done"], m + 1)
                    dve.wait_ge(s["hc_done"], m + 1)
                    flat = (a[p][:].rearrange("p i c t -> p (i c t)") for a in (hs, da, dbx))
                    nc.vector.tensor_tensor_scan(*flat, 0.0, ALU.mult, ALU.add).then_inc(s["h_done"], 1)

                def pair(k, p):
                    inputs(k + 1, 1 - p)
                    states(k, p)

                if k0 == 0:
                    inputs(0, 0)
                if k1 < NP:
                    repeat(dve, k0, k1, pair)
                elif k1 - k0 > RING:
                    repeat(dve, k0, k1 - RING, pair)
                    pair(NP - 2, 0)
                    states(NP - 1, 1)
                else:
                    for k in range(k0, k1 - 1):
                        pair(k, k % RING)
                    states(NP - 1, 1)

            def gate_out(layer, b):
                dve.wait_ge(s["y_done"], NP * (b + 1) + RING)
                nc.vector.tensor_tensor(yz[b][:], y_sum, sz2[:, :, b, :], ALU.mult).then_inc(s["yz_ready"], 1)

            def out_norm(layer, b):
                dve.wait_ge(s["o_ps"], b + 1)
                link(clamp(norm_a[b][:], m_tok))
                batch_statistics(b, norm_a[b], 1e-5, "var3")

            def skip_norm(layer, b):
                link(normalise(TT, norm_b[b], norm_a[b], mv[b], rstd[b], "rstd3", b))
                link(clamp(norm_b[b][:], norm_b[b][:]))
                link(nc.vector.tensor_tensor(t_tok[b][:], x_tok[:, TT * b:TT * (b + 1), :], norm_b[b][:], ALU.add))
                batch_statistics(b, t_tok[b], 1e-5, "var4")

            def inner_norm(layer, b):
                link(normalise(TT, xn_tok[b], t_tok[b], mv[b], rstd[b], "rstd4", b))
                link(nc.vector.tensor_tensor(veps[b][:], rstd[b][:], rstd[b][:], ALU.mult))
                link(nc.vector.tensor_tensor(veps[b][:], veps[b][:], mv[b][:, :, 1], ALU.mult))
                nc.vector.tensor_scalar(veps[b][:], veps[b][:], 1e-5, None, ALU.add).then_inc(s["var5"], 1)
                link(nc.vector.tensor_tensor(t_tok[b][:], t_tok[b][:], xn_tok[b][:], ALU.add))

            def inner_scale(layer, b):
                if layer == 0:
                    dve.wait_ge(s["rstd5"], b + 1)
                    for t in range(TT):
                        ins = nc.vector.tensor_scalar(xg_tok[b][:, t, :], xn_tok[b][:, t, :], rstd_b[b][:, t:t + 1], None, ALU.mult)
                else:
                    ins = normalise(TT, xg_tok[b], acc[NB + b], mv[b], rstd[b], "rstd7", b)
                ins.then_inc(s["xn_tok"], 1)

            def expert_in(layer, b):
                k = NB * layer + b
                dve.wait_ge(s["xn_ps"], k + 1)
                if layer == 0:
                    link(nc.vector.tensor_scalar(x_full[b][:], m_ps[:, 0:T], col("ln_g"), col("ln_b"), ALU.mult, ALU.add))
                else:
                    link(nc.vector.tensor_copy(x_full[b][:], m_ps[:, 0:T]))
                dve.sem_inc(s["x_full"], 1)
                link(nc.vector.tensor_copy(x_hi[b][:], x_full[b][:]))
                nc.vector.tensor_tensor(x_lo[b][:], x_full[b][:], x_hi[b][:].bitcast(F32), ALU.subtract).then_inc(s["xsplit"], 1)

            def logit_max(layer, b):
                wide = [128, TT, EXPERTS[layer]]
                logits = m_ps[:, 0:TT * EXPERTS[layer]].rearrange("p (t e) -> p t e", t=TT)
                dve.wait_ge(s["logit_ps"], NB * layer + b + 1)
                link(nc.vector.tensor_reduce(out=mx[b][:], in_=logits, op=ALU.max, axis=AX.X))
                nc.vector.tensor_tensor(z_sub[layer][b][:], logits,
                                        mx[b][:].rearrange("p (t o) -> p t o", o=1).to_broadcast(wide),
                                        ALU.subtract).then_inc(s["z_sub"], 1)

            def softmax(layer, b):
                n = EXPERTS[layer]
                th, den, root = z_exp[layer][b], z_den[layer][b], z_sub[layer][b]
                dve.wait_ge(s["z_tanh"], NB * layer + b + 1)
                link(nc.vector.tensor_scalar(den[:], th[:], -1.0, 1.0, ALU.mult, ALU.add))
                link(nc.vector.reciprocal(den[:], den[:]))
                link(nc.vector.scalar_tensor_tensor(root[:], th[:], 1.0, den[:], ALU.add, ALU.mult))
                link(nc.vector.tensor_tensor(th[:], root[:], root[:], ALU.mult))
                link(nc.vector.tensor_reduce(out=zsum[b][:], in_=th[:], op=ALU.add, axis=AX.X))
                link(nc.vector.reciprocal(zsum[b][:], zsum[b][:]))
                link(nc.vector.tensor_tensor(prob[layer][b][:, :, 0:n], th[:],
                                             zsum[b][:].rearrange("p (t o) -> p t o", o=1).to_broadcast([128, TT, n]), ALU.mult))

            def gates(layer, b):
                n = EXPERTS[layer]
                pr, rest_p = prob[layer][b], left[layer][b]
                for t in range(TT):
                    ins = nc.vector.max(top8[b][:, t, :], pr[:, t, :])
                link(ins)
                link(nc.vector.tensor_copy(top2[b][:, :, 0:TOPK], top8[b][:, :, 0:TOPK]))
                for t in range(TT):
                    ins = nc.vector.match_replace(out=rest_p[:, t, :], in_to_replace=top2[b][:, t, :],
                                                  in_values=pr[:, t, :], imm_value=0.0)
                link(ins)
                if layer == 0:
                    link(nc.vector.tensor_tensor(comb8[b][:], pr[:, :, 0:n], rest_p[:, :, 0:n], ALU.subtract))
                    nc.vector.tensor_copy(comb[0][b][:].rearrange("p t (e o) -> p t e o", o=UNITS // n),
                                          comb8[b][:].rearrange("p t (e o) -> p t e o", o=1).to_broadcast([128, TT, n, UNITS // n])
                                          ).then_inc(s["comb_ready"], 1)
                else:
                    nc.vector.tensor_tensor(comb[1][b][:], pr[:, :, 0:n], rest_p[:, :, 0:n], ALU.subtract).then_inc(s["comb_ready"], 1)

            def gates_tc(layer, b):
                dve.wait_ge(s["comb_ps"], b + 1)
                nc.vector.tensor_copy(combT[b][:], m_ps[0:EXPERTS[0], 0:T]).then_inc(s["combT_ready"], 1)

            def start_sum(layer, b):
                dve.wait_ge(s["b2_ps"], b + 1)
                nc.vector.tensor_tensor(acc[b][:], t_tok[b][:], m_tok, ALU.add).then_inc(s["acc_started"], 1)

            def experts(layer, b, u0, u1):
                k = NB * layer + b

                def unit(u, p):
                    dve.wait_ge(s["w2_done"], u + (UNITS * k + 1 + RING))
                    for t in range(TT):
                        dve.wait_ge(s["acc_done"], u * TT + (ACC * k + TT + t + 1))
                        nc.vector.scalar_tensor_tensor(acc[k][:, t, :], o_ps[:, p, 128 * t:128 * (t + 1)],
                                                       comb[layer][b][:, t, bass.ds(u, 1)], acc[k][:, t, :],
                                                       ALU.mult, ALU.add).then_inc(s["acc_done"], 1)

                if u0 == 0:
                    dve.wait_ge(s["comb_ready"], k + 1)
                    dve.wait_ge(s["acc_started"], k + 1)
                repeat(dve, u0, u1, unit)

            def mix_stats(layer, b):
                dve.wait_ge(s["acc_done"], ACC * (b + 1) + RING * TT)
                batch_statistics(b, acc[b], 1e-6, "var6")

            def mix_norm(layer, b):
                normalise(TT, norm_a[b], acc[b], mv[b], rstd[b], "rstd6", b).then_inc(s["lnc_tok"], 1)

            def mix_tc(layer, b):
                dve.wait_ge(s["lnc_ps"], b + 1)
                nc.vector.tensor_copy(lnc[b][:], m_ps[:, 0:T]).then_inc(s["lnc_ready"], 1)

            def mix_c(layer, b):
                dve.wait_ge(s["mix_ps"], b + 1)
                nc.vector.tensor_copy(mix[b], m_ps[:, T:2 * T]).then_inc(s["mix_ready"], 1)

            def mix_add(layer, b):
                k = NB + b
                dve.wait_ge(s["mixT_ps"], b + 1)
                nc.vector.tensor_tensor(acc[k][:], acc[b][:], m_tok, ALU.add).then_inc(s["acc_started"], 1)
                dve.wait_ge(s["acc_started"], k + 1)
                batch_statistics(b, acc[k], 1e-5, "var7")

            def store(layer, b):
                dve.wait_ge(s["out_ps"], b + 1)
                nc.vector.tensor_copy(out_sb[b][:], m_ps[:, 0:T]).then_inc(s["out_sb"], 1)

            does = {"project": project, "x_proj": x_proj, "step_size": step_size, "scan": scan, "gate_out": gate_out,
                    "out_norm": out_norm, "skip_norm": skip_norm, "inner_norm": inner_norm, "inner_scale": inner_scale,
                    "expert_in": expert_in, "logit_max": logit_max, "softmax": softmax, "top2": gates,
                    "gates_tc": gates_tc, "start_sum": start_sum, "experts": experts, "mix_stats": mix_stats,
                    "mix_norm": mix_norm, "mix_tc": mix_tc, "mix_c": mix_c, "mix_add": mix_add, "store": store}
            for step, *arg in plan:
                if step in does:
                    does[step](*arg)

        @block.tensor
        def _(pe):
            pe.sem_inc(s["h_ready"], RING)
            pe.sem_inc(s["w2_done"], RING)
            pe.sem_inc(s["y_done"], RING)

            def to_channels(dst, src):
                for t in range(TT):
                    ins = nc.tensor.transpose(dst[:, 128 * t:128 * (t + 1)], src[:, t, :], ident[:])
                return ins

            def to_tokens(dst, src):
                for t in range(TT):
                    ins = nc.tensor.transpose(dst[:, t, :], src[:, 128 * t:128 * (t + 1)], ident[:])
                return ins

            def project():
                pe.wait_ge(s["ident_ready"], 1)
                pe.wait_ge(s["x_loaded"], 16)
                for b in range(NB):
                    ins = to_tokens(xt_ps[:, T * b:T * (b + 1)].rearrange("p (t c) -> p t c", t=TT), x_cm[:, b, :])
                ins.then_inc(s["xt_ps"], 1)
                pe.wait_ge(s["xs_tok"], 1)
                for b in range(NB):
                    ins = to_channels(xs_ps[:, T * b:T * (b + 1)], xs_b[:, TT * b:TT * (b + 1), :])
                ins.then_inc(s["xs_ps"], 1)
                pe.wait_ge(s["xs_ready"], 1)
                for c in range(DC):
                    nc.tensor.matmul(xin_ps[:, c, :], col("in_w")[:, 128 * c:128 * (c + 1)], xs[:],
                                     start=True, stop=True).then_inc(s["xin_ps"], 1)
                for c in range(DC):
                    ins = nc.tensor.matmul(z_ps[:, c, :], col("in_w")[:, DI + 128 * c:DI + 128 * (c + 1)], xs[:],
                                           start=True, stop=True)
                ins.then_inc(s["z_ps"], 1)

            def x_proj():
                pe.wait_ge(s["xproj_ready"], 1)
                for c in range(DC):
                    pe.wait_ge(s["xc_ready"], c + 1)
                    ins = nc.tensor.matmul(xd_ps[0:XP, :], xproj_w[:, c, :], xc2[:, c], start=(c == 0), stop=(c == DC - 1))
                ins.then_inc(s["xdbl_ps"], 1)
                pe.wait_ge(s["rows_loaded"], 16)
                pe.wait_ge(s["dtr_ready"], 1)
                for c in range(DC):
                    ins = nc.tensor.matmul(dt_ps[:, c, :], dtw[DT0:XP + 1, 128 * c:128 * (c + 1)], dtr[DT0:XP + 1],
                                           start=True, stop=True)
                ins.then_inc(s["dt_ps"], 1)

            def scan(b, k0, k1):
                def spread(k, p):
                    m = k + NP * b
                    pe.wait_ge(s["dbx_done"], m + 1)
                    pe.wait_ge(s["cb_done"], m + 1)
                    for which in range(2):
                        for i in range(PAIR):
                            ins = nc.tensor.matmul(bc_ps[p][which][:, T * i:T * (i + 1)],
                                                   sel[:, bass.ds((k * PAIR + (i + NS * which)) * 128, 128)], parts[:, b, :],
                                                   start=True, stop=True)
                    ins.then_inc(s["bc_ready"], 1)

                def add(k, p, last=False):
                    pe.wait_ge(s["hc_done"], k + (NP * b + 1 + RING))
                    for i in range(PAIR):
                        ins = nc.tensor.matmul(y_ps, ident[:], hc[p][:, i], start=False, stop=(last and i == PAIR - 1))
                    ins.then_inc(s["y_done"], 1)

                def pair(k, p):
                    spread(k + RING, p)
                    add(k + (-1), 1 - p)

                if k0 == 0:
                    pe.wait_ge(s["sel_ready"], 1)
                    pe.wait_ge(s["parts_ready"], 1)
                    pe.wait_ge(s["sz_ready"], 1)
                    spread(0, 0)
                    spread(1, 1)
                    pe.wait_ge(s["diag_ready"], 1)
                    if b:
                        pe.wait_ge(s["yz_ready"], b)
                    for c in range(DC):
                        nc.tensor.matmul(y_sum[:, c, :], diag_d[:, c, :], xc2[:, c, b, :], start=(c == 0), stop=False)
                k = k0
                while k < k1:
                    if k == RING and k1 >= NP - RING:
                        repeat(pe, RING, NP - RING, pair)
                        k = NP - RING
                        continue
                    if k + RING < NP:
                        spread(k + RING, k % RING)
                    if k:
                        add(k - 1, (k - 1) % RING)
                    k += 1
                if k1 == NP:
                    add(NP - 1, (NP - 1) % RING, last=True)

            def out_proj(layer, b):
                pe.wait_ge(s["outw_ready"], 1)
                pe.wait_ge(s["yz_ready"], b + 1)
                for t in range(TT):
                    for c in range(DC):
                        ins = nc.tensor.matmul(m_tok[:, t, :], yz[b][:, c, 128 * t:128 * (t + 1)],
                                               outw_half[:, 128 * c:128 * (c + 1)], start=(c == 0), stop=(c == DC - 1))
                ins.then_inc(s["o_ps"], 1)

            def to_channel(layer, b):
                pe.wait_ge(s["xn_tok"], NB * layer + b + 1)
                to_channels(m_ps[:, 0:T], xg_tok[b]).then_inc(s["xn_ps"], 1)

            def logits(layer, b):
                n = EXPERTS[layer]
                pe.wait_ge(s["x_full"], NB * layer + b + 1)
                for t in range(TT):
                    ins = nc.tensor.matmul(m_ps[:, n * t:n * (t + 1)], x_full[b][:, 128 * t:128 * (t + 1)], col(f"gate{layer}"),
                                           start=True, stop=True)
                ins.then_inc(s["logit_ps"], 1)

            def gates_t(layer, b):
                pe.wait_ge(s["comb_ready"], b + 1)
                for t in range(TT):
                    ins = nc.tensor.transpose(m_ps[0:EXPERTS[0], 128 * t:128 * (t + 1)], comb8[b][:, t, :], ident[:])
                ins.then_inc(s["comb_ps"], 1)

            def bias2(layer, b):
                pe.wait_ge(s["b2_loaded"], 16)
                pe.wait_ge(s["combT_ready"], b + 1)
                for t in range(TT):
                    ins = nc.tensor.matmul(m_tok[:, t, :], combT[b][:, 128 * t:128 * (t + 1)], b2_sb[:], start=True, stop=True)
                ins.then_inc(s["b2_ps"], 1)

            def experts(layer, b, u0, u1):
                k = NB * layer + b

                def hidden(u, p):
                    pe.wait_ge(s["w1_staged"], u + (UNITS * k + 1))
                    pe.wait_ge(s["gelu_done"], u + (UNITS * k + 1))
                    for c in range(UC):
                        at = slice(128 * c, 128 * (c + 1))
                        nc.tensor.matmul(h_ps[:, p, T * c:T * (c + 1)], w1_hi[p][:, at], x_hi[b][:], start=True, stop=False)
                        nc.tensor.matmul(h_ps[:, p, T * c:T * (c + 1)], w1_hi[p][:, at], x_lo[b][:], start=False, stop=False)
                        ins = nc.tensor.matmul(h_ps[:, p, T * c:T * (c + 1)], w1_lo[p][:, at], x_hi[b][:], start=False, stop=True)
                    ins.then_inc(s["h_ready"], 1)

                def output(u, p):
                    pe.wait_ge(s["gelu_done"], u + (UNITS * k + 1 + RING))
                    pe.wait_ge(s["acc_done"], u * TT + (ACC * k + TT))
                    for t in range(TT):
                        for c in range(UC):
                            ins = nc.tensor.matmul(o_ps[:, p, 128 * t:128 * (t + 1)], hid[p][:, c, 128 * t:128 * (t + 1)],
                                                   w2[layer][:, bass.ds(u * UC + c, 1), :], start=(c == 0), stop=(c == UC - 1))
                    ins.then_inc(s["w2_done"], 1)

                def unit(u, p):
                    hidden(u + 1, 1 - p)
                    output(u, p)

                if u0 == 0:
                    pe.wait_ge(s["xsplit"], k + 1)
                    if b == 0:
                        pe.wait_ge(s[f"w2_{layer}_loaded"], 32)
                    hidden(0, 0)
                if u1 < UNITS:
                    repeat(pe, u0, u1, unit)
                else:
                    if u1 - u0 > RING:
                        repeat(pe, u0, u1 - RING, unit)
                        u0 = u1 - RING
                    for u in range(u0, u1 - 1):
                        unit(u, u % RING)
                    output(UNITS - 1, (UNITS - 1) % RING)

            def mix_t(layer, b):
                pe.wait_ge(s["lnc_tok"], b + 1)
                to_channels(m_ps[:, 0:T], norm_a[b]).then_inc(s["lnc_ps"], 1)

            def mix_pe(layer, b):
                pe.wait_ge(s["decay_ready"], 1)
                pe.wait_ge(s["lnc_ready"], b + 1)
                w = T // H
                for r in range(H):
                    ins = nc.tensor.matmul(m_ps[:, T + w * r:T + w * (r + 1)], decay_m[:, r, :], lnc[b][:, w * r:w * (r + 1)],
                                           start=True, stop=True)
                ins.then_inc(s["mix_ps"], 1)

            def mix_back(layer, b):
                pe.wait_ge(s["mix_ready"], b + 1)
                to_tokens(m_tok, mix[b]).then_inc(s["mixT_ps"], 1)

            def store_t(layer, b):
                pe.wait_ge(s["acc_done"], ACC * (NB + b + 1) + RING * TT)
                to_channels(m_ps[:, 0:T], acc[NB + b]).then_inc(s["out_ps"], 1)

            does = {"project": project, "x_proj": x_proj, "scan": scan, "out_proj": out_proj, "to_channel": to_channel,
                    "logits": logits, "gates_t": gates_t, "bias2": bias2, "experts": experts, "mix_t": mix_t,
                    "mix": mix_pe, "mix_back": mix_back, "store_t": store_t}
            for step, *arg in plan:
                if step in does:
                    does[step](*arg)


def repeat(engine, first, end, unit):
    start = min(first + first % RING, end)
    loops = (end - start) // RING
    for u in range(first, start):
        unit(u, u % RING)
    if loops > 1:
        with engine.Fori(0, loops) as i:
            for p in range(RING):
                unit(i * RING + (start + p), p)
        start += loops * RING
    for u in range(start, end):
        unit(u, u % RING)


def kernel(x, L0_conv_norm_w, L0_conv_norm_b, L0_conv_in_proj_w, L0_conv_conv_w, L0_conv_conv_b, L0_conv_x_proj_w,
           L0_conv_dt_proj_w, L0_conv_dt_proj_b, L0_conv_A_log, L0_conv_D, L0_conv_out_proj_w, L0_ffn_gate_w,
           L0_ffn_w1, L0_ffn_b1, L0_ffn_w2, L0_ffn_b2, L0_ffn_ln_g, L0_ffn_ln_b, L1_conv_A, L1_ffn_W_gate,
           L1_ffn_W1, L1_ffn_W2):
    import concourse.bacc as bacc
    from concourse.bass_utils import run_bass_kernel_spmd

    def chunks(a):
        a = np.asarray(a).reshape(-1, 128, np.asarray(a).size // np.asarray(a).shape[0])
        return a.transpose(1, 0, 2).reshape(128, -1)

    parts = {"in_w": np.asarray(L0_conv_in_proj_w).T, "out_w": chunks(np.asarray(L0_conv_out_proj_w).T),
             "xproj": chunks(np.asarray(L0_conv_x_proj_w).T), "conv_b": chunks(L0_conv_conv_b),
             "conv_w": chunks(np.asarray(L0_conv_conv_w).reshape(DI, TAPS)),
             "a_log": chunks(L0_conv_A_log), "d_skip": chunks(L0_conv_D), "norm_w": chunks(L0_conv_norm_w),
             "norm_b": chunks(L0_conv_norm_b), "ln_g": chunks(L0_ffn_ln_g), "ln_b": chunks(L0_ffn_ln_b),
             "gate0": np.asarray(L0_ffn_gate_w), "gate1": np.asarray(L1_ffn_W_gate),
             "b1": chunks(np.asarray(L0_ffn_b1).reshape(-1))}
    arrays = {
        "x_in": np.asarray(x).reshape(NB, C, T),
        "packed_in": np.concatenate([parts[name] for name in COLS], axis=1),
        "dt_rows_in": np.concatenate([np.asarray(L0_conv_dt_proj_w).T, np.asarray(L0_conv_dt_proj_b).reshape(1, DI)]),
        "w1_0_in": np.asarray(L0_ffn_w1), "w2_0_in": np.asarray(L0_ffn_w2), "b2_in": np.asarray(L0_ffn_b2),
        "decay_in": np.asarray(L1_conv_A).reshape(1, H),
        "w1_1_in": np.asarray(L1_ffn_W1), "w2_1_in": np.asarray(L1_ffn_W2),
    }
    arrays = {name: np.ascontiguousarray(a) for name, a in arrays.items()}
    nc = bacc.Bacc("TRN2", target_bir_lowering=False, num_devices=1)
    ap = {name: nc.dram_tensor(name, a.shape, mybir.dt.from_np(a.dtype), kind="ExternalInput").ap()
          for name, a in arrays.items()}
    y = nc.dram_tensor("y_out", (NB, C, T), F32, kind="ExternalOutput").ap()
    bass_metaformer(nc, ap["x_in"].rearrange("b c t -> c b t"), ap["packed_in"], ap["dt_rows_in"],
                    ap["w1_0_in"], ap["w2_0_in"], ap["b2_in"], ap["decay_in"].to_broadcast([128, H]),
                    ap["w1_1_in"], ap["w2_1_in"], y.rearrange("b c t -> c b t"))
    r = run_bass_kernel_spmd(nc, [arrays], core_ids=[0])
    return r.results[0]["y_out"].reshape(NB, C, H, T // H)
```

```python
from contextlib import ExitStack

import numpy as np

import concourse.bass as bass
from concourse import mybir

F32 = mybir.dt.float32
F32R = mybir.dt.float32r
BF16 = mybir.dt.bfloat16
ALU = mybir.AluOpType
ACT = mybir.ActivationFunctionType
AX = mybir.AxisListType

NB = 2
C = 128
H = 16
T = 256
TT = T // 128
DI = 256
DC = DI // 128
NS = 16
TAPS = 4
DTR = 8
BC = 2 * NS
SPLIT = 3
XP = SPLIT * BC + DTR
DT0 = SPLIT * BC
EXPERTS = (8, 16)
UNITS = 16
UW = 256
UC = UW // 128
TOPK = 2
CLAMP = 10.0
RING = 2
PAIR = 2
NP = NS // PAIR
WARM_PAIR = 4
PASSES = 2 * NB
ACC = TT * UNITS

COLS = {}
_at = 0
for _name, _width in (("in_w", 2 * DI), ("out_w", DC * C), ("xproj", DC * (DTR + BC)), ("conv_b", DC), ("conv_w", DC * TAPS),
                      ("a_log", DC * NS), ("d_skip", DC), ("norm_w", 1), ("norm_b", 1), ("ln_g", 1),
                      ("ln_b", 1), ("gate0", EXPERTS[0]), ("gate1", EXPERTS[1]), ("b1", UNITS * UC)):
    COLS[_name] = (_at, _at + _width)
    _at += _width
PACKED = _at

SEMS = """
x_loaded params_loaded rows_loaded decay_loaded b2_loaded w1_0_loaded w2_0_loaded w1_1_loaded w2_1_loaded
ident_ready one_ready sel_ready xproj_ready outw_ready a_exp a_ready diag_ready
pool_chain dve_chain act_chain
xt_ps var1 rstd1 var2 rstd2 xs_tok xs_ps xs_ready xin_ps z_ps tap_ready u_ready th_u th_z xc_ready sz_ready
xdbl_ps dtr_ready high_ready parts_ready dt_ps exp_dt onep_dt rounding_dt ln_dt log1p_ready dt_ready dtx_ready gate_ready
bc_ready dbx_done cb_done da_done h_done hc_done y_done
yz_ready o_ps var3 rstd3 var4 rstd4 xn_ready t_ready rstd5 xn_tok xn_ps x_full x_hi_ready xsplit logit_ps z_sub z_tanh comb_ready
comb_ps combT_ready b2_ps
w1_hi_done w1_staged h_ready gelu_done w2_done acc_started acc_done
var6 rstd6 var7 rstd7
out_ps out_sb out_stored
""".split()


def bass_metaformer(nc, x, packed, dt_rows, w1_0, w2_0, b2, decay, w1_1, w2_1, out):
    with ExitStack() as ctx:
        def sb(name, shape, dt=F32):
            return ctx.enter_context(nc.sbuf_tensor(name, shape, dt))

        def per_batch(name, shape, dt=F32):
            return [sb(f"{name}_{b}", shape, dt) for b in range(NB)]

        x_cm = sb("x_cm", [C, NB, T])
        par = sb("par", [C, PACKED])
        dtw = sb("dtw", [128, DI])
        b2_sb = sb("b2_sb", [EXPERTS[0], C])
        decay_sb = sb("decay_sb", [128, TT])
        w1 = [sb("w1a", [C, UNITS * UW]), sb("w1b", [C, UNITS * UW])]
        w2 = [sb("w2a", [128, UNITS * UC, C]), sb("w2b", [128, UNITS * UC, C])]

        def col(name):
            return par[:, COLS[name][0]:COLS[name][1]]

        ident = sb("ident", [128, 128])
        sel_id = sb("sel_id", [SPLIT * BC, BC], BF16)
        sel = sb("sel", [SPLIT * BC, BC * 128], BF16)
        neg_half = sb("neg_half", [128, 1])
        one = sb("one", [128, 1])
        xproj_w = sb("xproj_w", [128, DC, XP])
        outw_half = sb("outw_half", [128, DC * C])
        a_neg = sb("a_neg", [128, DC * NS])
        diag_d = sb("diag_d", [128, DC, 128])

        x_tok = sb("x_tok", [128, NB * TT, C])
        xs_a = sb("xs_a", [128, NB * TT, C])
        xs_b = sb("xs_b", [128, NB * TT, C])
        xs = sb("xs", [C, NB, T])
        u2 = sb("u2", [128, DC, NB, T])
        th_u = sb("th_u", [128, DC, NB, T])
        th_z = sb("th_z", [128, DC, NB, T])
        xc2 = sb("xc2", [128, DC, NB, T])
        sz2 = sb("sz2", [128, DC, NB, T])
        zc = sb("zc", [128, DC, NB, T])
        rest = xs_a[0:SPLIT * BC].rearrange("p (b t) c -> p b (t c)", b=NB)
        mid = sb("mid", [SPLIT * BC, NB, T], BF16)
        parts = sb("parts", [SPLIT * BC, NB, T], BF16)
        dtr = sb("dtr", [128, NB, T])
        dt_e = th_u
        dt_l = u2
        dt_w = sz2
        dt = sb("dt", [128, DC, NB, T])
        dtx = per_batch("dtx", [128, DC, T])
        da = [sb(f"da_{p}", [128, PAIR, DC, T]) for p in range(RING)]
        dbx = [sb(f"dbx_{p}", [128, PAIR, DC, T]) for p in range(RING)]
        hs = [sb(f"hs_{p}", [128, PAIR, DC, T]) for p in range(RING)]
        cb = [sb(f"cb_{p}", [128, PAIR, T]) for p in range(RING)]
        hc = [sb(f"hc_{p}", [128, PAIR, DC, T]) for p in range(RING)]
        yz = dtx

        stats = per_batch("stats", [128, TT, 6])
        mv = per_batch("mv", [128, TT, 2])
        veps = per_batch("veps", [128, TT])
        rstd = per_batch("rstd", [128, TT])
        rstd_b = per_batch("rstd_b", [128, TT])
        norm_a = per_batch("norm_a", [128, TT, C])
        norm_b = per_batch("norm_b", [128, TT, C])
        t_tok = per_batch("t_tok", [128, TT, C])
        xn_tok = per_batch("xn_tok", [128, TT, C])
        xg_tok = per_batch("xg_tok", [128, TT, C])
        x_full = per_batch("x_full", [C, T])
        x_hi = per_batch("x_hi", [C, T], F32R)
        x_lo = per_batch("x_lo", [C, T], F32R)
        mx = per_batch("mx", [128, TT])
        z_sub = [[sb(f"z_sub_{l}_{b}", [128, TT, EXPERTS[l]]) for b in range(NB)] for l in range(2)]
        z_den = [[sb(f"z_den_{l}_{b}", [128, TT, EXPERTS[l]]) for b in range(NB)] for l in range(2)]
        z_exp = [[sb(f"z_exp_{l}_{b}", [128, TT, EXPERTS[l]]) for b in range(NB)] for l in range(2)]
        prob = [[sb(f"prob_{l}_{b}", [128, TT, EXPERTS[l] + 8]) for b in range(NB)] for l in range(2)]
        left = [[sb(f"left_{l}_{b}", [128, TT, EXPERTS[l] + 8]) for b in range(NB)] for l in range(2)]
        top8 = per_batch("top8", [128, TT, 8])
        top2 = per_batch("top2", [128, TT, 8])
        zsum = per_batch("zsum", [128, TT])
        comb8 = per_batch("comb8", [128, TT, EXPERTS[0]])
        comb = [[sb(f"comb_{l}_{b}", [128, TT, UNITS]) for b in range(NB)] for l in range(2)]
        combT = per_batch("combT", [EXPERTS[0], T])
        w1_hi = [sb(f"w1_hi_{p}", [C, UW], F32R) for p in range(RING)]
        w1_lo = [sb(f"w1_lo_{p}", [C, UW], F32R) for p in range(RING)]
        hid = [sb(f"hid_{p}", [128, UC, T]) for p in range(RING)]
        acc = [sb(f"acc_{k}", [128, TT, C]) for k in range(2 * NB)]
        out_sb = per_batch("out_sb", [C, T])

        def banks(name, n):
            return ctx.enter_context(nc.psum_tensor(name, [128, n, 512], F32))

        b_ps, h_ps, o_ps = banks("b_ps", RING), banks("h_ps", RING), banks("o_ps", RING)
        y_ps, m_ps = banks("y_ps", 1)[:, 0, :], banks("m_ps", 1)[:, 0, :]
        m_tok = m_ps[:, 0:T].rearrange("p (t c) -> p t c", t=TT)
        y_bank = [m_ps, y_ps]
        y_sum = [a.rearrange("p (c t) -> p c t", c=DC) for a in y_bank]

        xt_ps = xin_ps = [b_ps[:, 0, :], b_ps[:, 1, :]]
        xs_ps = z_ps = [h_ps[:, 0, :], h_ps[:, 1, :]]
        xd_ps = [o_ps[:, 0, :], m_ps]
        dt_ps = [o_ps[:, 1, :], y_ps]

        def halves(bank):
            return bank.rearrange("p (c t) -> p c t", c=DC)

        bc_ps = [(b_ps[:, p, :], o_ps[:, p, :]) for p in range(RING)]

        s = {name: ctx.enter_context(nc.semaphore(name)) for name in SEMS}
        block = ctx.enter_context(nc.Block())

        in_scan = [["gate_factors"], ["gate_out"], ["out_proj", "out_norm", "root_3"], ["skip_norm", "skip_stats", "root_4"],
                   ["inner_norm", "root_5"], ["inner_scale"], ["to_channel"], ["expert_in", "logits", "logit_max"]]
        routed = [["to_channel"], ["expert_in"], ["logits", "logit_max"], ["softmax"], ["gates"]]
        in_experts = [[], [], ["gate_out"], ["out_proj", "out_norm"], ["root_3", "skip_norm"], ["skip_stats"],
                      ["root_4", "inner_norm"], ["root_5"], ["inner_scale"]] + routed + [["gates_t", "gates_tc"],
                      ["bias2", "start_sum"]]
        mixer = [["mix_stats"], ["root_6", "mix_norm"], ["mix_add"], ["root_7", "inner_scale"]] + routed

        def between(work, end, groups, layer, b):
            plan = []
            singles = min(len(groups) + len(groups) % RING, end)
            for k in range(singles):
                plan.append((*work, k, k + 1))
                plan += [(name, layer, b) for name in (groups[k] if k < len(groups) else [])]
            return plan + ([(*work, singles, end)] if singles < end else [])

        plan = [("constants",)]
        for stage in ("x_stats", "x_norm", "inner_x", "in_proj", "conv", "silu", "x_proj", "softplus", "log"):
            plan += [(stage, b) for b in range(NB)]
        plan += [("step_size", 0), ("step_size", 1), ("gate", 0), ("scan", 0, 0, RING), ("scan", 0, RING, NP)]
        plan += between(("scan", 1), NP, in_scan, 0, 0)
        plan += [("experts", 0, 0, 0, 1), ("last_sum",), ("softmax", 0, 0), ("gates", 0, 0), ("gates_t", 0, 0),
                 ("gates_tc", 0, 0), ("start_sum", 0, 0), ("experts", 0, 0, 1, 2), ("gate", 1)]
        plan += between(("experts", 0, 0), UNITS, in_experts, 0, 1)[2:]
        plan += between(("experts", 0, 1), UNITS, mixer, 1, 0)
        plan += between(("experts", 1, 0), UNITS, mixer, 1, 1)
        plan += between(("experts", 1, 1), UNITS, [["store_t"], ["store"]], 1, 0)
        plan += [("store_t", 1, 1), ("store", 1, 1)]

        @block.sync
        def _(sp):
            sp.dma_start(x_cm[:], x).then_inc(s["x_loaded"], 16)
            sp.dma_start(par[:], packed).then_inc(s["params_loaded"], 16)
            sp.dma_start(dtw[DT0:DT0 + DTR + 1, :], dt_rows).then_inc(s["rows_loaded"], 16)
            sp.dma_start(decay_sb[:], decay).then_inc(s["decay_loaded"], 16)
            sp.dma_start(b2_sb[:], b2).then_inc(s["b2_loaded"], 16)
            for layer, (w1_d, w2_d) in enumerate(((w1_0, w2_0), (w1_1, w2_1))):
                n = EXPERTS[layer] // 2
                fw = UNITS * UW // EXPERTS[layer]
                w1_v = w1[layer][:].rearrange("c (e f) -> c e f", f=fw)
                for i in range(2):
                    sp.dma_start(w1_v[:, n * i:n * (i + 1), :],
                                 w1_d[n * i:n * (i + 1)].rearrange("e c f -> c e f")).then_inc(s[f"w1_{layer}_loaded"], 16)
                    m = UNITS * UC // 2
                    sp.dma_start(w2[layer][:, m * i:m * (i + 1), :],
                                 w2_d.rearrange("e (j p) c -> p (e j) c", p=128)[:, m * i:m * (i + 1), :]
                                 ).then_inc(s[f"w2_{layer}_loaded"], 16)
            for b in range(NB):
                sp.wait_ge(s["out_sb"], b + 1)
                sp.dma_start(out[:, b, :], out_sb[b][:]).then_inc(s["out_stored"], 16)
            sp.wait_ge(s["out_stored"], 16 * NB)

        @block.gpsimd
        def _(pool):
            chain = [0]

            def link(ins):
                chain[0] += 1
                ins.then_inc(s["pool_chain"], 1)
                pool.wait_ge(s["pool_chain"], chain[0])

            def rsqrt(dst, var, eps, done):
                link(nc.gpsimd.tensor_scalar(dst, var, eps, None, ALU.add))
                nc.gpsimd.tensor_tensor(dst, dst, neg_half[:, 0:1].to_broadcast(list(dst.shape)), ALU.pow).then_inc(s[done], 1)

            pool.sem_inc(s["hc_done"], RING)
            link(nc.gpsimd.memset(ident[:], 0.0))
            nc.gpsimd.affine_select(out=ident[:], in_=ident[:], compare_op=ALU.not_equal, fill=1.0, base=0,
                                    pattern=[[-1, 128]], channel_multiplier=1).then_inc(s["ident_ready"], 1)
            link(nc.gpsimd.memset(neg_half[:], -0.5))
            link(nc.gpsimd.memset(one[:], 1.0))
            pool.sem_inc(s["one_ready"], 1)
            link(nc.gpsimd.memset(sel_id[:], 0.0))
            for j in range(SPLIT):
                link(nc.gpsimd.affine_select(out=sel_id[:], in_=sel_id[:], compare_op=ALU.not_equal, fill=1.0,
                                             base=-BC * j, pattern=[[-1, BC]], channel_multiplier=1))
            link(nc.gpsimd.memset(dtr[DT0:DT0 + 32, :, :], 1.0))
            for b in range(NB):
                link(nc.gpsimd.memset(da[b][:, :, :, 0:1], 0.0))
                link(nc.gpsimd.memset(top2[b][:], -1.0))
                for layer in range(2):
                    link(nc.gpsimd.memset(prob[layer][b][:], -1.0))

            def weights_and_selectors():
                pool.wait_ge(s["params_loaded"], 16)
                link(nc.gpsimd.tensor_scalar(outw_half[:], col("out_w"), 0.5, None, ALU.mult))
                pool.sem_inc(s["outw_ready"], 1)
                pool.wait_ge(s["a_exp"], 1)
                nc.gpsimd.tensor_scalar(a_neg[:], a_neg[:], -1.0, None, ALU.mult).then_inc(s["a_ready"], 1)
                nc.gpsimd.tensor_scalar(sel[:].rearrange("k (n m) -> k n m", m=128),
                                        sel_id[:].rearrange("k (n o) -> k n o", o=1).to_broadcast([SPLIT * BC, BC, 128]),
                                        1.0, None, ALU.mult).then_inc(s["sel_ready"], 1)

            def scan(b, k0, k1):
                def pair(k, p):
                    m = k + NP * b
                    pool.wait_ge(s["h_done"], m + (1 + RING))
                    pool.wait_ge(s["cb_done"], m + (1 + RING))
                    pool.wait_ge(s["y_done"], m + 1)
                    nc.gpsimd.tensor_tensor(hc[p][:], hs[p][:],
                                            cb[p][:].rearrange("p i (o t) -> p i o t", o=1).to_broadcast([128, PAIR, DC, T]),
                                            ALU.mult).then_inc(s["hc_done"], 1)

                repeat(pool, k0, k1, pair)

            def low_part(k, u, p):
                layer = k // NB
                pool.wait_ge(s[f"w1_{layer}_loaded"], 32)
                pool.wait_ge(s["w1_hi_done"], u + (UNITS * k + 1))
                nc.gpsimd.tensor_tensor(w1_lo[p][:], w1[layer][:, bass.ds(u * UW, UW)], w1_hi[p][:].bitcast(F32),
                                        ALU.subtract).then_inc(s["w1_staged"], 1)

            def experts(layer, b, u0, u1):
                k = NB * layer + b
                end = min(u1, UNITS - RING)
                if u0 < end:
                    repeat(pool, u0 + RING, end + RING, lambda u, p: low_part(k, u, p))
                for u in range(max(u0, end), u1):
                    if k + 1 < PASSES:
                        low_part(k + 1, u + RING - UNITS, u % RING)

            def step_size(b):
                if b == 0:
                    return
                e, ln = dt_e[:, :, b, :], dt_l[:, :, b, :]
                pool.wait_ge(s["rounding_dt"], b + 1)
                pool.wait_ge(s["ln_dt"], b + 1)
                nc.gpsimd.tensor_tensor(ln, ln, e, ALU.subtract).then_inc(s["log1p_ready"], 1)
                pool.wait_ge(s["dt_ready"], b + 1)
                nc.gpsimd.tensor_tensor(dtx[b][:], xc2[:, :, b, :], dt[:, :, b, :], ALU.mult).then_inc(s["dtx_ready"], 1)

            def gate(b):
                pool.wait_ge(s["gate_ready"], b + 1)
                pool.wait_ge(s["rounding_dt"], b + 1)
                nc.gpsimd.tensor_tensor(sz2[:, :, b, :], th_z[:, :, b, :], zc[:, :, b, :], ALU.mult).then_inc(s["sz_ready"], 1)

            def root_5(layer, b):
                pool.wait_ge(s["rstd4"], b + 1)
                link(nc.gpsimd.tensor_tensor(veps[b][:], rstd[b][:], rstd[b][:], ALU.mult))
                link(nc.gpsimd.tensor_tensor(veps[b][:], veps[b][:], mv[b][:, :, 1], ALU.mult))
                rsqrt(rstd_b[b][:], veps[b][:], 1e-5, "rstd5")

            def start_sum(layer, b):
                pool.wait_ge(s["xn_ready"], b + 1)
                nc.gpsimd.tensor_tensor(t_tok[b][:], t_tok[b][:], xn_tok[b][:], ALU.add).then_inc(s["t_ready"], 1)

            roots = {"x_stats": ("1", 1e-6), "x_norm": ("2", 1e-5), "root_3": ("3", 1e-5), "root_4": ("4", 1e-5),
                     "root_6": ("6", 1e-6), "root_7": ("7", 1e-5)}
            for step, *arg in plan:
                if step in roots:
                    b = arg[-1]
                    which, eps = roots[step]
                    pool.wait_ge(s["var" + which], b + 1)
                    rsqrt((rstd_b if which == "2" else rstd)[b][:], mv[b][:, :, 1], eps, "rstd" + which)
                    if (step, b) == ("x_norm", NB - 1):
                        weights_and_selectors()
                elif step == "root_5":
                    root_5(*arg)
                elif (step, *arg) == ("log", NB - 1):
                    for u in range(RING):
                        low_part(0, u, u)
                elif step == "step_size":
                    step_size(*arg)
                elif step == "gate":
                    gate(*arg)
                elif step == "logit_max" and arg[0] == 0:
                    start_sum(*arg)
                elif step == "scan":
                    scan(*arg)
                elif step == "experts":
                    experts(*arg)

        @block.scalar
        def _(act):
            chain = [0]

            def link(ins):
                chain[0] += 1
                ins.then_inc(s["act_chain"], 1)
                act.wait_ge(s["act_chain"], chain[0])

            act.sem_inc(s["cb_done"], RING)
            act.sem_inc(s["gelu_done"], RING)

            def constants():
                act.wait_ge(s["params_loaded"], 16)
                nc.scalar.activation(a_neg[:], col("a_log"), ACT.Exp).then_inc(s["a_exp"], 1)

            def conv(b):
                act.wait_ge(s["xin_ps"], b + 1)
                taps = col("conv_w").rearrange("p (c k) -> p c k", c=DC)
                for c in range(DC):
                    nc.scalar.activation(u2[:, c, b, :], halves(xin_ps[b])[:, c, :], ACT.Identity,
                                         scale=taps[:, c, TAPS - 1:TAPS], bias=col("conv_b")[:, c:c + 1]).then_inc(s["tap_ready"], 1)

            def silu(b):
                act.wait_ge(s["u_ready"], DC * (b + 1))
                nc.scalar.activation(th_u[:, :, b, :], u2[:, :, b, :], ACT.Tanh, scale=0.5).then_inc(s["th_u"], 1)
                act.wait_ge(s["z_ps"], b + 1)
                nc.scalar.activation(th_z[:, :, b, :], halves(z_ps[b]), ACT.Tanh, scale=0.5).then_inc(s["th_z"], 1)

            def x_proj(b):
                act.wait_ge(s["xdbl_ps"], b + 1)
                nc.scalar.activation(dtr[DT0:XP, b, :], xd_ps[b][DT0:XP, 0:T], ACT.Copy).then_inc(s["dtr_ready"], 1)
                nc.scalar.activation(parts[:, b, :], xd_ps[b][0:SPLIT * BC, 0:T], ACT.Copy).then_inc(s["high_ready"], 1)
                if b == NB - 1:
                    for u in range(RING):
                        high_part(0, u, u)

            def softplus(b):
                act.wait_ge(s["dt_ps"], b + 1)
                link(nc.scalar.activation(dt_w[:, :, b, :], halves(dt_ps[b]), ACT.Abs))
                nc.scalar.activation(dt_e[:, :, b, :], dt_w[:, :, b, :], ACT.Exp, scale=-1.0).then_inc(s["exp_dt"], 1)

            def log(b):
                act.wait_ge(s["onep_dt"], b + 1)
                nc.scalar.activation(dt_l[:, :, b, :], dt_w[:, :, b, :], ACT.Ln).then_inc(s["ln_dt"], 1)
                if b == NB - 1:
                    gate_factors(0)

            def gate_factors(b):
                act.wait_ge(s["one_ready"], 1)
                act.wait_ge(s["th_z"], b + 1)
                nc.scalar.activation(th_z[:, :, b, :], th_z[:, :, b, :], ACT.Identity, bias=one[:, 0:1])
                nc.scalar.activation(zc[:, :, b, :], halves(z_ps[b]), ACT.Copy).then_inc(s["gate_ready"], 1)

            def scan(b, k0, k1):
                def pair(k, p):
                    m = k + NP * b
                    act.wait_ge(s["h_done"], m + 1)
                    for i in range(PAIR):
                        for c in range(DC):
                            ins = nc.scalar.activation(da[p][:, i, c, 1:T], dt[:, c, b, 1:T], ACT.Exp,
                                                       scale=a_neg[:, bass.ds(k * PAIR + (c * NS + i), 1)])
                    ins.then_inc(s["da_done"], 1)
                    act.wait_ge(s["bc_ready"], m + 1)
                    act.wait_ge(s["hc_done"], m + 1)
                    nc.scalar.activation(cb[p][:], bc_ps[p][1].rearrange("p (i t) -> p i t", i=PAIR),
                                         ACT.Copy).then_inc(s["cb_done"], 1)

                if k0 == 0:
                    act.wait_ge(s["a_ready"], 1)
                    act.wait_ge(s["dt_ready"], b + 1)
                repeat(act, k0, k1, pair)

            def expert_in(layer, b):
                k = NB * layer + b
                act.wait_ge(s["xn_ps"], k + 1)
                if layer == 0:
                    ins = nc.scalar.activation(x_full[b][:], m_ps[:, 0:T], ACT.Identity, scale=col("ln_g"), bias=col("ln_b"))
                else:
                    ins = nc.scalar.activation(x_full[b][:], m_ps[:, 0:T], ACT.Copy)
                ins.then_inc(s["x_full"], 1)
                act.wait_ge(s["x_full"], k + 1)
                nc.scalar.activation(x_hi[b][:], x_full[b][:], ACT.Copy).then_inc(s["x_hi_ready"], 1)

            def softmax(layer, b):
                act.wait_ge(s["z_sub"], NB * layer + b + 1)
                nc.scalar.activation(z_exp[layer][b][:], z_sub[layer][b][:], ACT.Tanh, scale=0.25).then_inc(s["z_tanh"], 1)

            def high_part(k, u, p):
                layer = k // NB
                act.wait_ge(s[f"w1_{layer}_loaded"], 32)
                nc.scalar.activation(w1_hi[p][:], w1[layer][:, bass.ds(u * UW, UW)], ACT.Copy).then_inc(s["w1_hi_done"], 1)

            def gelu(k, u, p):
                act.wait_ge(s["h_ready"], u + (UNITS * k + 1 + RING))
                act.wait_ge(s["w2_done"], u + (UNITS * k + 1))
                if k < NB:
                    for c in range(UC):
                        at = COLS["b1"][0] + c
                        ins = nc.scalar.activation(hid[p][:, c, :], h_ps[:, p, T * c:T * (c + 1)], ACT.Gelu,
                                                   bias=par[:, bass.ds(u * UC + at, 1)])
                else:
                    ins = nc.scalar.activation(hid[p][:], h_ps[:, p, :].rearrange("p (c t) -> p c t", c=UC), ACT.Gelu)
                ins.then_inc(s["gelu_done"], 1)

            def experts(layer, b, u0, u1):
                k = NB * layer + b

                def unit(u, p):
                    gelu(k, u, p)
                    high_part(k, u + RING, p)

                end = min(u1, UNITS - RING)
                if u0 < end:
                    repeat(act, u0, end, unit)
                for u in range(max(u0, end), u1):
                    gelu(k, u, u % RING)
                    if k + 1 < PASSES:
                        high_part(k + 1, u + RING - UNITS, u % RING)

            does = {"constants": constants, "conv": conv, "silu": silu, "x_proj": x_proj, "softplus": softplus, "log": log,
                    "gate_factors": lambda layer, b: gate_factors(NB - 1), "scan": scan, "expert_in": expert_in,
                    "softmax": softmax, "experts": experts}
            for step, *arg in plan:
                if step in does:
                    does[step](*arg)

        @block.vector
        def _(dve):
            chain = [0]

            def link(ins):
                chain[0] += 1
                ins.then_inc(s["dve_chain"], 1)
                dve.wait_ge(s["dve_chain"], chain[0])

            dve.sem_inc(s["dbx_done"], RING)
            dve.sem_inc(s["h_done"], RING)
            dve.sem_inc(s["acc_done"], RING * TT)

            def statistics(n, src, stats, mv, done):
                for t in range(n):
                    ins = nc.vector.bn_stats(stats[:, t, :], src[:, t, :])
                link(ins)
                for t in range(n):
                    ins = nc.vector.bn_aggr(mv[:, t, :], stats[:, t, :])
                ins.then_inc(s[done], 1)

            def batch_statistics(b, src, done):
                statistics(TT, src, stats[b], mv[b], done)

            def normalise(n, dst, src, mv, root, root_sem, k):
                dve.wait_ge(s[root_sem], k + 1)
                for t in range(n):
                    ins = nc.vector.tensor_scalar(dst[:, t, :], src[:, t, :], mv[:, t, 0:1], root[:, t:t + 1],
                                                  ALU.subtract, ALU.mult)
                return ins

            def clamp(dst, src):
                return nc.vector.tensor_scalar(dst, src, CLAMP, -CLAMP, ALU.min, ALU.max)

            def constants():
                dve.wait_ge(s["params_loaded"], 16)
                wx = col("xproj").rearrange("p (c r) -> p c r", c=DC)
                copies = xproj_w[:, :, 0:DT0].rearrange("p c (j r) -> p c j r", j=SPLIT)
                for at, half in ((slice(0, NS), 0.25), (slice(NS, BC), 0.5)):
                    rows = wx[:, :, DTR + at.start:DTR + at.stop].rearrange("p c (o r) -> p c o r", o=1)
                    nc.vector.tensor_scalar(copies[:, :, :, at], rows.to_broadcast([128, DC, SPLIT, NS]), half, None, ALU.mult)
                nc.vector.tensor_scalar(xproj_w[:, :, DT0:XP], wx[:, :, 0:DTR], 0.5, None, ALU.mult).then_inc(s["xproj_ready"], 1)
                dve.wait_ge(s["ident_ready"], 1)
                for c in range(DC):
                    ins = nc.vector.tensor_scalar(diag_d[:, c, :], ident[:], col("d_skip")[:, c:c + 1], 0.5, ALU.mult, ALU.mult)
                ins.then_inc(s["diag_ready"], 1)
                dve.wait_ge(s["decay_loaded"], 16)
                link(nc.vector.tensor_scalar(decay_sb[:], decay_sb[:], 1e-6, None, ALU.max))

            def x_stats(b):
                at = slice(TT * b, TT * (b + 1))
                dve.wait_ge(s["xt_ps"], b + 1)
                link(nc.vector.tensor_copy(x_tok[:, at, :], xt_ps[b][:, 0:T].rearrange("p (t c) -> p t c", t=TT)))
                batch_statistics(b, x_tok[:, at, :], "var1")

            def x_norm(b):
                at = slice(TT * b, TT * (b + 1))
                link(normalise(TT, xs_a[:, at, :], x_tok[:, at, :], mv[b], rstd[b], "rstd1", b))
                link(clamp(xs_a[:, at, :], xs_a[:, at, :]))
                batch_statistics(b, xs_a[:, at, :], "var2")

            def inner_x(b):
                at = slice(TT * b, TT * (b + 1))
                normalise(TT, xs_b[:, at, :], xs_a[:, at, :], mv[b], rstd_b[b], "rstd2", b).then_inc(s["xs_tok"], 1)

            def in_proj(b):
                dve.wait_ge(s["xs_ps"], b + 1)
                link(nc.vector.tensor_scalar(xs[:, b, :], xs_ps[b][:, 0:T], col("norm_w"), col("norm_b"), ALU.mult, ALU.add))
                clamp(xs[:, b, :], xs[:, b, :]).then_inc(s["xs_ready"], 1)

            def conv(b):
                taps = col("conv_w").rearrange("p (c k) -> p c k", c=DC)
                last = [0] * DC
                dve.wait_ge(s["tap_ready"], DC * (b + 1))
                for back in range(1, TAPS):
                    for c in range(DC):
                        if back > 1:
                            dve.wait_ge(s["dve_chain"], last[c])
                        ins = nc.vector.scalar_tensor_tensor(u2[:, c, b, back:T], halves(xin_ps[b])[:, c, 0:T - back],
                                                             taps[:, c, TAPS - 1 - back:TAPS - back],
                                                             u2[:, c, b, back:T], ALU.mult, ALU.add)
                        if back < TAPS - 1:
                            chain[0] += 1
                            last[c] = chain[0]
                            ins.then_inc(s["dve_chain"], 1)
                        else:
                            ins.then_inc(s["u_ready"], 1)

            def silu(b):
                dve.wait_ge(s["u_ready"], DC * (b + 1))
                dve.wait_ge(s["th_u"], b + 1)
                nc.vector.scalar_tensor_tensor(xc2[:, :, b, :], th_u[:, :, b, :], 1.0, u2[:, :, b, :],
                                               ALU.add, ALU.mult).then_inc(s["xc_ready"], 1)

            def x_proj(b):
                rows, n = xd_ps[b][:, 0:T], SPLIT * BC
                dve.wait_ge(s["high_ready"], b + 1)
                link(nc.vector.tensor_tensor(rest[:, b, :], rows[0:n], parts[:, b, :], ALU.subtract))
                nc.vector.tensor_copy(parts[BC:2 * BC, b, :], rest[BC:2 * BC, b, :])
                link(nc.vector.tensor_copy(mid[2 * BC:n, b, :], rest[2 * BC:n, b, :]))
                nc.vector.tensor_tensor(parts[2 * BC:n, b, :], rest[2 * BC:n, b, :], mid[2 * BC:n, b, :],
                                        ALU.subtract).then_inc(s["parts_ready"], 1)

            def softplus(b):
                w, e = dt_w[:, :, b, :], dt_e[:, :, b, :]
                dve.wait_ge(s["exp_dt"], b + 1)
                nc.vector.tensor_scalar(w, e, 1.0, None, ALU.add).then_inc(s["onep_dt"], 1)
                dve.wait_ge(s["onep_dt"], b + 1)
                nc.vector.scalar_tensor_tensor(e, w, -1.0, e, ALU.add, ALU.subtract).then_inc(s["rounding_dt"], 1)

            def step_size(b):
                e, ln = dt_e[:, :, b, :], dt_l[:, :, b, :]
                if b == 0:
                    dve.wait_ge(s["rounding_dt"], 1)
                    dve.wait_ge(s["ln_dt"], 1)
                    link(nc.vector.tensor_tensor(ln, ln, e, ALU.subtract))
                else:
                    dve.wait_ge(s["log1p_ready"], 1)
                nc.vector.scalar_tensor_tensor(dt[:, :, b, :], halves(dt_ps[b]), 0.0, ln, ALU.max, ALU.add).then_inc(s["dt_ready"], 1)
                if b == 0:
                    dve.wait_ge(s["dt_ready"], 1)
                    link(nc.vector.tensor_tensor(dtx[b][:], xc2[:, :, b, :], dt[:, :, b, :], ALU.mult))

            def scan(b, k0, k1):
                def inputs(b, k, p):
                    m = k + NP * b
                    if b:
                        dve.wait_ge(s["dtx_ready"], 1)
                    dve.wait_ge(s["h_done"], m + 1)
                    dve.wait_ge(s["bc_ready"], m + 1)
                    rows = bc_ps[p][0].rearrange("p (i o t) -> p i o t", i=PAIR, o=1)
                    nc.vector.tensor_tensor(dbx[p][:], dtx[b][:].rearrange("p (o c) t -> p o c t", o=1).to_broadcast([128, PAIR, DC, T]),
                                            rows.to_broadcast([128, PAIR, DC, T]), ALU.mult).then_inc(s["dbx_done"], 1)

                def states(k, p):
                    m = k + NP * b
                    dve.wait_ge(s["dbx_done"], m + (1 + RING))
                    dve.wait_ge(s["da_done"], m + 1)
                    dve.wait_ge(s["hc_done"], m + 1)
                    flat = (a[p][:].rearrange("p i c t -> p (i c t)") for a in (hs, da, dbx))
                    nc.vector.tensor_tensor_scan(*flat, 0.0, ALU.mult, ALU.add).then_inc(s["h_done"], 1)

                def pair(k, p):
                    inputs(b, k + 1, 1 - p)
                    states(k, p)

                if b == 0 and k0 == 0:
                    inputs(0, 0, 0)
                repeat(dve, k0, min(k1, NP - 1), pair)
                if k1 == NP:
                    if b + 1 < NB:
                        inputs(b + 1, 0, 0)
                    states(NP - 1, (NP - 1) % RING)

            def gate_out(layer, b):
                dve.wait_ge(s["y_done"], NP * (b + 1) + RING)
                dve.wait_ge(s["sz_ready"], b + 1)
                nc.vector.tensor_tensor(yz[b][:], y_sum[b], sz2[:, :, b, :], ALU.mult).then_inc(s["yz_ready"], 1)

            def out_norm(layer, b):
                dve.wait_ge(s["o_ps"], b + 1)
                link(clamp(norm_a[b][:], m_tok))
                batch_statistics(b, norm_a[b], "var3")

            def skip_norm(layer, b):
                link(normalise(TT, norm_b[b], norm_a[b], mv[b], rstd[b], "rstd3", b))
                link(clamp(norm_b[b][:], norm_b[b][:]))
                link(nc.vector.tensor_tensor(t_tok[b][:], x_tok[:, TT * b:TT * (b + 1), :], norm_b[b][:], ALU.add))

            def skip_stats(layer, b):
                batch_statistics(b, t_tok[b], "var4")

            def inner_norm(layer, b):
                normalise(TT, xn_tok[b], t_tok[b], mv[b], rstd[b], "rstd4", b).then_inc(s["xn_ready"], 1)

            def inner_scale(layer, b):
                if layer == 0:
                    dve.wait_ge(s["xn_ready"], b + 1)
                    dve.wait_ge(s["rstd5"], b + 1)
                    for t in range(TT):
                        ins = nc.vector.tensor_scalar(xg_tok[b][:, t, :], xn_tok[b][:, t, :], rstd_b[b][:, t:t + 1], None, ALU.mult)
                else:
                    ins = normalise(TT, xg_tok[b], acc[NB + b], mv[b], rstd[b], "rstd7", b)
                ins.then_inc(s["xn_tok"], 1)

            def expert_in(layer, b):
                dve.wait_ge(s["x_hi_ready"], NB * layer + b + 1)
                nc.vector.tensor_tensor(x_lo[b][:], x_full[b][:], x_hi[b][:].bitcast(F32), ALU.subtract).then_inc(s["xsplit"], 1)

            def logit_max(layer, b):
                wide = [128, TT, EXPERTS[layer]]
                logits = m_ps[:, 0:TT * EXPERTS[layer]].rearrange("p (t e) -> p t e", t=TT)
                dve.wait_ge(s["logit_ps"], NB * layer + b + 1)
                link(nc.vector.tensor_reduce(out=mx[b][:], in_=logits, op=ALU.max, axis=AX.X))
                nc.vector.tensor_tensor(z_sub[layer][b][:], logits,
                                        mx[b][:].rearrange("p (t o) -> p t o", o=1).to_broadcast(wide),
                                        ALU.subtract).then_inc(s["z_sub"], 1)

            def softmax(layer, b):
                n = EXPERTS[layer]
                th, den, root = z_exp[layer][b], z_den[layer][b], z_sub[layer][b]
                dve.wait_ge(s["z_tanh"], NB * layer + b + 1)
                link(nc.vector.tensor_scalar(den[:], th[:], -1.0, 1.0, ALU.mult, ALU.add))
                link(nc.vector.reciprocal(den[:], den[:]))
                link(nc.vector.scalar_tensor_tensor(root[:], th[:], 1.0, den[:], ALU.add, ALU.mult))
                link(nc.vector.tensor_tensor(th[:], root[:], root[:], ALU.mult))
                link(nc.vector.tensor_reduce(out=zsum[b][:], in_=th[:], op=ALU.add, axis=AX.X))
                link(nc.vector.reciprocal(zsum[b][:], zsum[b][:]))
                link(nc.vector.tensor_tensor(prob[layer][b][:, :, 0:n], th[:],
                                             zsum[b][:].rearrange("p (t o) -> p t o", o=1).to_broadcast([128, TT, n]), ALU.mult))

            def gates(layer, b):
                n = EXPERTS[layer]
                pr, rest_p = prob[layer][b], left[layer][b]
                for t in range(TT):
                    ins = nc.vector.max(top8[b][:, t, :], pr[:, t, :])
                link(ins)
                link(nc.vector.tensor_copy(top2[b][:, :, 0:TOPK], top8[b][:, :, 0:TOPK]))
                for t in range(TT):
                    ins = nc.vector.match_replace(out=rest_p[:, t, :], in_to_replace=top2[b][:, t, :],
                                                  in_values=pr[:, t, :], imm_value=0.0)
                link(ins)
                if layer == 0:
                    link(nc.vector.tensor_tensor(comb8[b][:], pr[:, :, 0:n], rest_p[:, :, 0:n], ALU.subtract))
                    nc.vector.tensor_copy(comb[0][b][:].rearrange("p t (e o) -> p t e o", o=UNITS // n),
                                          comb8[b][:].rearrange("p t (e o) -> p t e o", o=1).to_broadcast([128, TT, n, UNITS // n])
                                          ).then_inc(s["comb_ready"], 1)
                else:
                    nc.vector.tensor_tensor(comb[1][b][:], pr[:, :, 0:n], rest_p[:, :, 0:n], ALU.subtract).then_inc(s["comb_ready"], 1)

            def gates_tc(layer, b):
                dve.wait_ge(s["comb_ps"], b + 1)
                nc.vector.tensor_copy(combT[b][:], m_ps[0:EXPERTS[0], 0:T]).then_inc(s["combT_ready"], 1)

            def start_sum(layer, b):
                dve.wait_ge(s["b2_ps"], b + 1)
                dve.wait_ge(s["t_ready"], b + 1)
                nc.vector.tensor_tensor(acc[b][:], t_tok[b][:], m_tok, ALU.add).then_inc(s["acc_started"], 1)

            def experts(layer, b, u0, u1):
                k = NB * layer + b

                def unit(u, p):
                    dve.wait_ge(s["w2_done"], u + (UNITS * k + 1 + RING))
                    for t in range(TT):
                        dve.wait_ge(s["acc_done"], u * TT + (ACC * k + TT + t + 1))
                        nc.vector.scalar_tensor_tensor(acc[k][:, t, :], o_ps[:, p, 128 * t:128 * (t + 1)],
                                                       comb[layer][b][:, t, bass.ds(u, 1)], acc[k][:, t, :],
                                                       ALU.mult, ALU.add).then_inc(s["acc_done"], 1)

                first, end = max(u0 - 1, 0), (u1 if u1 == UNITS else u1 - 1)
                if first == 0 and end > 0:
                    dve.wait_ge(s["comb_ready"], k + 1)
                    dve.wait_ge(s["acc_started"], k + 1)
                repeat(dve, first, end, unit)

            def mix_stats(layer, b):
                dve.wait_ge(s["acc_done"], ACC * (b + 1) + RING * TT)
                batch_statistics(b, acc[b], "var6")

            def mix_norm(layer, b):
                link(normalise(TT, norm_a[b], acc[b], mv[b], rstd[b], "rstd6", b))
                for t in range(TT):
                    ins = nc.vector.tensor_tensor_scan(norm_b[b][:, t, :], decay_sb[:, t:t + 1].to_broadcast([128, C]),
                                                       norm_a[b][:, t, :], 0.0, ALU.mult, ALU.add)
                link(ins)

            def mix_add(layer, b):
                k = NB + b
                nc.vector.tensor_tensor(acc[k][:], acc[b][:], norm_b[b][:], ALU.add).then_inc(s["acc_started"], 1)
                dve.wait_ge(s["acc_started"], k + 1)
                batch_statistics(b, acc[k], "var7")

            def store(layer, b):
                dve.wait_ge(s["out_ps"], b + 1)
                nc.vector.tensor_copy(out_sb[b][:], m_ps[:, 0:T]).then_inc(s["out_sb"], 1)

            does = {"x_stats": x_stats, "x_norm": x_norm, "inner_x": inner_x, "in_proj": in_proj, "conv": conv,
                    "silu": silu, "x_proj": x_proj, "softplus": softplus, "step_size": step_size, "scan": scan, "gate_out": gate_out,
                    "out_norm": out_norm, "skip_norm": skip_norm, "skip_stats": skip_stats, "inner_norm": inner_norm, "inner_scale": inner_scale,
                    "expert_in": expert_in, "logit_max": logit_max, "softmax": softmax, "gates": gates,
                    "gates_tc": gates_tc, "start_sum": start_sum, "experts": experts, "mix_stats": mix_stats,
                    "mix_norm": mix_norm, "mix_add": mix_add, "store": store}
            for step, *arg in plan:
                if step in does:
                    does[step](*arg)
                if (step, *arg) == ("x_stats", NB - 1):
                    constants()

        @block.tensor
        def _(pe):
            pe.sem_inc(s["h_ready"], RING)
            pe.sem_inc(s["w2_done"], RING)
            pe.sem_inc(s["y_done"], RING)

            def to_channels(dst, src):
                for t in range(TT):
                    ins = nc.tensor.transpose(dst[:, 128 * t:128 * (t + 1)], src[:, t, :], ident[:])
                return ins

            def to_tokens(dst, src):
                for t in range(TT):
                    ins = nc.tensor.transpose(dst[:, t, :], src[:, 128 * t:128 * (t + 1)], ident[:])
                return ins

            def keep_warm(sem, value, n=3, bank=m_ps):
                pe.wait_ge(s[sem], value)
                for _ in range(n):
                    nc.tensor.matmul(bank[:, 0:128], ident[:], ident[:], start=True, stop=True)

            def idle_products(n):
                for _ in range(n):
                    nc.tensor.matmul(h_ps[:, 0, 0:128], ident[:], ident[:], start=True, stop=True)

            def x_stats(b):
                if b == 0:
                    keep_warm("ident_ready", 1)
                pe.wait_ge(s["ident_ready"], 1)
                pe.wait_ge(s["x_loaded"], 16)
                to_tokens(xt_ps[b][:, 0:T].rearrange("p (t c) -> p t c", t=TT), x_cm[:, b, :]).then_inc(s["xt_ps"], 1)

            def inner_x(b):
                if b == 0:
                    for sem, value in (("var1", 1), ("var1", 2), ("rstd1", 2), ("var2", 1), ("var2", 2)):
                        keep_warm(sem, value)
                pe.wait_ge(s["xs_tok"], b + 1)
                to_channels(xs_ps[b][:, 0:T], xs_b[:, TT * b:TT * (b + 1), :]).then_inc(s["xs_ps"], 1)

            def in_proj(b):
                pe.wait_ge(s["xs_ready"], b + 1)
                for bank, done in ((0, "xin_ps"), (1, "z_ps")):
                    for c in range(DC):
                        ins = nc.tensor.matmul((xin_ps, z_ps)[bank][b][:, T * c:T * (c + 1)],
                                               col("in_w")[:, DI * bank + 128 * c:DI * bank + 128 * (c + 1)], xs[:, b, :],
                                               start=True, stop=True)
                    ins.then_inc(s[done], 1)

            def silu(b):
                if b == 0:
                    keep_warm("tap_ready", DC * NB, 6)
                pe.wait_ge(s["xproj_ready"], 1)
                pe.wait_ge(s["xc_ready"], b + 1)
                for c in range(DC):
                    ins = nc.tensor.matmul(xd_ps[b][0:XP, 0:T], xproj_w[:, c, :], xc2[:, c, b, :], start=(c == 0), stop=(c == DC - 1))
                ins.then_inc(s["xdbl_ps"], 1)

            def x_proj(b):
                pe.wait_ge(s["rows_loaded"], 16)
                pe.wait_ge(s["dtr_ready"], b + 1)
                for c in range(DC):
                    ins = nc.tensor.matmul(dt_ps[b][:, T * c:T * (c + 1)], dtw[DT0:XP + 1, 128 * c:128 * (c + 1)],
                                           dtr[DT0:XP + 1, b, :], start=True, stop=True)
                ins.then_inc(s["dt_ps"], 1)

            def spread(b, k, p):
                m = k + NP * b
                pe.wait_ge(s["dbx_done"], m + 1)
                pe.wait_ge(s["cb_done"], m + 1)
                for which in range(2):
                    for i in range(PAIR):
                        ins = nc.tensor.matmul(bc_ps[p][which][:, T * i:T * (i + 1)],
                                               sel[:, bass.ds((k * PAIR + (i + NS * which)) * 128, 128)], parts[:, b, :],
                                               start=True, stop=True)
                ins.then_inc(s["bc_ready"], 1)

            def add(b, k, p, last=False):
                pe.wait_ge(s["hc_done"], k + (NP * b + 1 + RING))
                for i in range(PAIR):
                    ins = nc.tensor.matmul(y_bank[b], ident[:], hc[p][:, i], start=False, stop=(last and i == PAIR - 1))
                ins.then_inc(s["y_done"], 1)

            def scan(b, k0, k1):
                def pair(k, p):
                    add(b, k + (-RING), p)
                    spread(b, k + RING, p)
                    if b and k0 >= WARM_PAIR:
                        idle_products(6)

                if b == 0 and k0 == 0:
                    for sem, value in (("parts_ready", NB), ("exp_dt", 1), ("onep_dt", NB), ("ln_dt", 1), ("ln_dt", NB)):
                        keep_warm(sem, value, 4)
                    pe.wait_ge(s["sel_ready"], 1)
                    pe.wait_ge(s["parts_ready"], 1)
                    pe.wait_ge(s["dt_ready"], 1)
                    for k in range(RING):
                        spread(0, k, k)
                    pe.wait_ge(s["diag_ready"], 1)
                for k in range(k0, min(k1, RING)):
                    if b:
                        add(b - 1, NP - RING + k, k, last=(k == RING - 1))
                    if k == RING - 1:
                        pe.wait_ge(s["parts_ready"], NB)
                        if b:
                            pe.wait_ge(s["dt_ready"], NB)
                        for c in range(DC):
                            nc.tensor.matmul(y_sum[b][:, c, :], diag_d[:, c, :], xc2[:, c, b, :], start=(c == 0), stop=False)
                    if b == 0 and k == 0:
                        keep_warm("dt_ready", NB, 4, bank=y_ps)
                        keep_warm("dbx_done", 1 + RING, 4, bank=y_ps)
                    spread(b, k + RING, k)
                    if b == 0 and k == 0:
                        keep_warm("cb_done", 1 + RING, 4, bank=y_ps)
                first, end = max(k0, RING), min(k1, NP - RING)
                if first < end:
                    repeat(pe, first, end, pair)
                for k in range(max(k0, NP - RING), k1):
                    add(b, k - RING, k % RING)
                    if b + 1 < NB:
                        spread(b + 1, k + RING - NP, k % RING)

            def last_sum():
                add(NB - 1, NP - 1, (NP - 1) % RING, last=True)

            def out_proj(layer, b):
                pe.wait_ge(s["outw_ready"], 1)
                pe.wait_ge(s["yz_ready"], b + 1)
                for t in range(TT):
                    for c in range(DC):
                        ins = nc.tensor.matmul(m_tok[:, t, :], yz[b][:, c, 128 * t:128 * (t + 1)],
                                               outw_half[:, 128 * c:128 * (c + 1)], start=(c == 0), stop=(c == DC - 1))
                ins.then_inc(s["o_ps"], 1)

            def to_channel(layer, b):
                pe.wait_ge(s["xn_tok"], NB * layer + b + 1)
                to_channels(m_ps[:, 0:T], xg_tok[b]).then_inc(s["xn_ps"], 1)

            def logits(layer, b):
                n = EXPERTS[layer]
                pe.wait_ge(s["x_full"], NB * layer + b + 1)
                for t in range(TT):
                    ins = nc.tensor.matmul(m_ps[:, n * t:n * (t + 1)], x_full[b][:, 128 * t:128 * (t + 1)], col(f"gate{layer}"),
                                           start=True, stop=True)
                ins.then_inc(s["logit_ps"], 1)

            def gates_t(layer, b):
                pe.wait_ge(s["comb_ready"], b + 1)
                for t in range(TT):
                    ins = nc.tensor.transpose(m_ps[0:EXPERTS[0], 128 * t:128 * (t + 1)], comb8[b][:, t, :], ident[:])
                ins.then_inc(s["comb_ps"], 1)

            def bias2(layer, b):
                pe.wait_ge(s["b2_loaded"], 16)
                pe.wait_ge(s["combT_ready"], b + 1)
                for t in range(TT):
                    ins = nc.tensor.matmul(m_tok[:, t, :], combT[b][:, 128 * t:128 * (t + 1)], b2_sb[:], start=True, stop=True)
                ins.then_inc(s["b2_ps"], 1)

            def experts(layer, b, u0, u1):
                k = NB * layer + b

                def hidden(u, p):
                    pe.wait_ge(s["w1_staged"], u + (UNITS * k + 1))
                    pe.wait_ge(s["gelu_done"], u + (UNITS * k + 1))
                    for c in range(UC):
                        at = slice(128 * c, 128 * (c + 1))
                        nc.tensor.matmul(h_ps[:, p, T * c:T * (c + 1)], w1_hi[p][:, at], x_hi[b][:], start=True, stop=False)
                        nc.tensor.matmul(h_ps[:, p, T * c:T * (c + 1)], w1_hi[p][:, at], x_lo[b][:], start=False, stop=False)
                        ins = nc.tensor.matmul(h_ps[:, p, T * c:T * (c + 1)], w1_lo[p][:, at], x_hi[b][:], start=False, stop=True)
                    ins.then_inc(s["h_ready"], 1)

                def output(u, p):
                    pe.wait_ge(s["gelu_done"], u + (UNITS * k + 1 + RING))
                    pe.wait_ge(s["acc_done"], u * TT + (ACC * k + TT))
                    for t in range(TT):
                        for c in range(UC):
                            ins = nc.tensor.matmul(o_ps[:, p, 128 * t:128 * (t + 1)], hid[p][:, c, 128 * t:128 * (t + 1)],
                                                   w2[layer][:, bass.ds(u * UC + c, 1), :], start=(c == 0), stop=(c == UC - 1))
                    ins.then_inc(s["w2_done"], 1)

                def unit(u, p):
                    hidden(u + 1, 1 - p)
                    if (k, u0, u1) == (0, 0, 1):
                        add(NB - 1, NP - RING, (NP - RING) % RING)
                    if (k, u0, u1) == (0, 1, 2):
                        bias2(layer, b)
                    output(u, p)

                if u0 == 0:
                    pe.wait_ge(s["xsplit"], k + 1)
                    if b == 0:
                        pe.wait_ge(s[f"w2_{layer}_loaded"], 32)
                    hidden(0, 0)
                if u1 < UNITS:
                    repeat(pe, u0, u1, unit)
                else:
                    if u1 - u0 > RING:
                        repeat(pe, u0, u1 - RING, unit)
                        u0 = u1 - RING
                    for u in range(u0, u1 - 1):
                        unit(u, u % RING)
                    output(UNITS - 1, (UNITS - 1) % RING)

            def store_t(layer, b):
                pe.wait_ge(s["acc_done"], ACC * (NB + b + 1) + RING * TT)
                to_channels(m_ps[:, 0:T], acc[NB + b]).then_inc(s["out_ps"], 1)

            does = {"x_stats": x_stats, "inner_x": inner_x, "in_proj": in_proj, "silu": silu, "x_proj": x_proj,
                    "scan": scan, "last_sum": last_sum, "out_proj": out_proj, "to_channel": to_channel, "logits": logits,
                     "gates_t": gates_t, "bias2": bias2, "experts": experts, "store_t": store_t}
            for step, *arg in plan:
                if step in does:
                    does[step](*arg)


def repeat(engine, first, end, unit):
    start = max(first, min(first + first % RING, end))
    loops = max(0, end - start) // RING
    for u in range(first, start):
        unit(u, u % RING)
    if loops > 1:
        with engine.Fori(0, loops) as i:
            for p in range(RING):
                unit(i * RING + (start + p), p)
        start += loops * RING
    for u in range(start, end):
        unit(u, u % RING)


def kernel(x, L0_conv_norm_w, L0_conv_norm_b, L0_conv_in_proj_w, L0_conv_conv_w, L0_conv_conv_b, L0_conv_x_proj_w,
           L0_conv_dt_proj_w, L0_conv_dt_proj_b, L0_conv_A_log, L0_conv_D, L0_conv_out_proj_w, L0_ffn_gate_w,
           L0_ffn_w1, L0_ffn_b1, L0_ffn_w2, L0_ffn_b2, L0_ffn_ln_g, L0_ffn_ln_b, L1_conv_A, L1_ffn_W_gate,
           L1_ffn_W1, L1_ffn_W2):
    import concourse.bacc as bacc
    from concourse.bass_utils import run_bass_kernel_spmd

    def chunks(a):
        a = np.asarray(a).reshape(-1, 128, np.asarray(a).size // np.asarray(a).shape[0])
        return a.transpose(1, 0, 2).reshape(128, -1)

    parts = {"in_w": np.asarray(L0_conv_in_proj_w).T, "out_w": chunks(np.asarray(L0_conv_out_proj_w).T),
             "xproj": chunks(np.asarray(L0_conv_x_proj_w).T), "conv_b": chunks(L0_conv_conv_b),
             "conv_w": chunks(np.asarray(L0_conv_conv_w).reshape(DI, TAPS)),
             "a_log": chunks(L0_conv_A_log), "d_skip": chunks(L0_conv_D), "norm_w": chunks(L0_conv_norm_w),
             "norm_b": chunks(L0_conv_norm_b), "ln_g": chunks(L0_ffn_ln_g), "ln_b": chunks(L0_ffn_ln_b),
             "gate0": np.asarray(L0_ffn_gate_w), "gate1": np.asarray(L1_ffn_W_gate),
             "b1": chunks(np.asarray(L0_ffn_b1).reshape(-1))}
    arrays = {
        "x_in": np.asarray(x).reshape(NB, C, T),
        "packed_in": np.concatenate([parts[name] for name in COLS], axis=1),
        "dt_rows_in": np.concatenate([np.asarray(L0_conv_dt_proj_w).T, np.asarray(L0_conv_dt_proj_b).reshape(1, DI)]),
        "w1_0_in": np.asarray(L0_ffn_w1), "w2_0_in": np.asarray(L0_ffn_w2), "b2_in": np.asarray(L0_ffn_b2),
        "decay_in": np.repeat(np.asarray(L1_conv_A), T // H).reshape(TT, 128).T,
        "w1_1_in": np.asarray(L1_ffn_W1), "w2_1_in": np.asarray(L1_ffn_W2),
    }
    arrays = {name: np.ascontiguousarray(a) for name, a in arrays.items()}
    nc = bacc.Bacc("TRN2", target_bir_lowering=False, num_devices=1)
    ap = {name: nc.dram_tensor(name, a.shape, mybir.dt.from_np(a.dtype), kind="ExternalInput").ap()
          for name, a in arrays.items()}
    y = nc.dram_tensor("y_out", (NB, C, T), F32, kind="ExternalOutput").ap()
    bass_metaformer(nc, ap["x_in"].rearrange("b c t -> c b t"), ap["packed_in"], ap["dt_rows_in"],
                    ap["w1_0_in"], ap["w2_0_in"], ap["b2_in"], ap["decay_in"],
                    ap["w1_1_in"], ap["w2_1_in"], y.rearrange("b c t -> c b t"))
    r = run_bass_kernel_spmd(nc, [arrays], core_ids=[0])
    return r.results[0]["y_out"].reshape(NB, C, H, T // H)
```
